# Optimizing a Trainium2 kernel written in Bass

```python
import numpy as np
import jax
import jax.numpy as jnp

def _softmax(x, axis=-1):
    return jax.nn.softmax(x, axis=axis)

def _gelu(x):
    return jax.nn.gelu(x, approximate=True)

def _silu(x):
    return jax.nn.silu(x)

def _sigmoid(x):
    return jax.nn.sigmoid(x)

def _layernorm(x, axis=-1, eps=1e-05):
    m = jnp.mean(x, axis=axis, keepdims=True)
    v = jnp.var(x, axis=axis, keepdims=True)
    return (x - m) / jnp.sqrt(v + eps)

def _scatter_add(tgt, idx, src, axis=0):
    return tgt.at[idx].add(src)

def _segment_sum(src, seg, n):
    return jax.ops.segment_sum(src, seg, n)
kernel_name = 'mk_seq_preln_d4_jaxref_r8_e041a4'

def setup_inputs(seed: int=0):
    np.random.seed(seed)
    _w = jnp.asarray

    def _L0_attn_setup():
        import jax, jax.numpy as jnp
        import numpy as np
        D = 128
        ROT = D // 2
        B, S = (4, 1024)

        def _l2norm(x, eps=1e-06):
            return x * jax.lax.rsqrt(jnp.sum(x * x, axis=-1, keepdims=True) + eps)

        def _rotary(x, rot_dim):
            seq = x.shape[-2]
            half = rot_dim // 2
            inv_freq = 1.0 / 10000.0 ** (jnp.arange(0, rot_dim, 2, dtype=jnp.float32) / rot_dim)
            freqs = jnp.arange(seq, dtype=jnp.float32)[:, None] * inv_freq[None, :]
            freqs = jnp.repeat(freqs, 2, axis=-1)
            cos, sin = (jnp.cos(freqs), jnp.sin(freqs))
            xr, xp = (x[..., :rot_dim], x[..., rot_dim:])
            x2 = xr.reshape(*xr.shape[:-1], half, 2)
            rh = jnp.stack([-x2[..., 1], x2[..., 0]], axis=-1).reshape(xr.shape)
            return jnp.concatenate([xr * cos + rh * sin, xp], axis=-1)

        def _layernorm(x, g, b, eps=1e-05):
            mu = jnp.mean(x, axis=-1, keepdims=True)
            var = jnp.mean(jnp.square(x - mu), axis=-1, keepdims=True)
            return (x - mu) * jax.lax.rsqrt(var + eps) * g + b
        key = jax.random.key(seed)
        k1, k2, k3 = jax.random.split(key, 3)
        X = jax.random.normal(k1, (B, S, D), jnp.float32)
        W_in = jax.random.normal(k2, (3 * D, D), jnp.float32) / np.float32(np.sqrt(D))
        W_out = jax.random.normal(k3, (D, D), jnp.float32) / np.float32(np.sqrt(D))
        ln_g = jnp.ones((D,), jnp.float32)
        ln_b = jnp.zeros((D,), jnp.float32)
        return {'X': X, 'W_in': W_in, 'W_out': W_out, 'ln_g': ln_g, 'ln_b': ln_b}
    _L0_attn_in = _L0_attn_setup()

    def _L0_ffn_setup():
        import jax, jax.numpy as jnp
        import numpy as np
        NUM_EXPERTS = 8
        D_MODEL = 128
        D_OUT = 128
        key = jax.random.key(seed)
        ks = jax.random.split(key, 5)
        B, S = (2, 256)
        x = jax.random.normal(ks[0], (B, S, D_MODEL), dtype=jnp.float32)
        gate_w = jax.random.normal(ks[1], (D_MODEL, NUM_EXPERTS), dtype=jnp.float32) * 0.02
        gate_b = jnp.zeros((NUM_EXPERTS,), dtype=jnp.float32)
        expert_w = jax.random.normal(ks[2], (NUM_EXPERTS, D_MODEL, D_OUT), dtype=jnp.float32) * 0.02
        expert_b = jnp.zeros((NUM_EXPERTS, D_OUT), dtype=jnp.float32)
        return {'x': x, 'gate_w': gate_w, 'gate_b': gate_b, 'expert_w': expert_w, 'expert_b': expert_b}
    _L0_ffn_in = _L0_ffn_setup()

    def _L1_attn_setup():
        import jax, jax.numpy as jnp
        import numpy as np
        import math
        EMB = 128
        HEADS = 16
        B, S = (2, 256)
        key = jax.random.key(seed)
        k_x, k_wq, k_bq, k_wu, k_bu = jax.random.split(key, 5)
        lim = 1.0 / math.sqrt(EMB)
        x = jax.random.normal(k_x, (B, S, EMB), dtype=jnp.float32)
        wq = jax.random.uniform(k_wq, (EMB, EMB), jnp.float32, -lim, lim)
        bq = jax.random.uniform(k_bq, (EMB,), jnp.float32, -lim, lim)
        wu = jax.random.uniform(k_wu, (EMB, EMB), jnp.float32, -lim, lim)
        bu = jax.random.uniform(k_bu, (EMB,), jnp.float32, -lim, lim)
        return {'x': x, 'wq': wq, 'bq': bq, 'wu': wu, 'bu': bu}
    _L1_attn_in = _L1_attn_setup()

    def _L1_ffn_setup():
        import jax, jax.numpy as jnp
        import numpy as np
        D = 128
        H = 16
        FF = 512
        E = 8
        K = 2
        EH = 128
        B, S = (2, 256)
        EPS = 1e-05

        def rmsnorm(x, w):
            v = jnp.mean(jnp.square(x), axis=-1, keepdims=True)
            return x * jax.lax.rsqrt(v + EPS) * w

        def _dense_path(x, wq, wk, wv, wo, w1, w2, w3, attn_norm_w, ff_norm_w):
            b, s, d = x.shape
            hd = d // H
            q = (x @ wq).reshape(b, s, H, hd)
            k = (x @ wk).reshape(b, s, H, hd)
            v = (x @ wv).reshape(b, s, H, hd)
            scores = jnp.einsum('bqhd,bkhd->bhqk', q, k) / np.sqrt(hd).astype(np.float32)
            causal = jnp.tril(jnp.ones((s, s), bool))
            scores = jnp.where(causal, scores, jnp.finfo(scores.dtype).min)
            attn = jax.nn.softmax(scores, axis=-1)
            o = jnp.einsum('bhqk,bkhd->bqhd', attn, v).reshape(b, s, d)
            h = x + rmsnorm(o @ wo, attn_norm_w)
            ffn = jax.nn.silu(h @ w1) * (h @ w3) @ w2
            return h + rmsnorm(ffn, ff_norm_w)

        def _sparse_path(x, router_w, ew1, ew2, ew3, moe_norm_w):
            b, s, d = x.shape
            xt = x.reshape(-1, d)
            probs = jax.nn.softmax(xt @ router_w, axis=-1)
            topw, topi = jax.lax.top_k(probs, K)
            g = jax.nn.silu(jnp.einsum('td,edh->eth', xt, ew1)) * jnp.einsum('td,edh->eth', xt, ew3)
            eo = jnp.einsum('eth,ehd->ted', g, ew2)
            sel = jnp.take_along_axis(eo, topi[:, :, None], axis=1)
            moe_out = jnp.sum(topw[:, :, None] * sel, axis=1).reshape(b, s, d)
            return rmsnorm(moe_out, moe_norm_w)
        key = jax.random.key(seed)
        ks = jax.random.split(key, 16)
        s = 0.02
        return {'x': jax.random.normal(ks[0], (B, S, D), jnp.float32), 'wq': jax.random.normal(ks[1], (D, D), jnp.float32) * s, 'wk': jax.random.normal(ks[2], (D, D), jnp.float32) * s, 'wv': jax.random.normal(ks[3], (D, D), jnp.float32) * s, 'wo': jax.random.normal(ks[4], (D, D), jnp.float32) * s, 'w1': jax.random.normal(ks[5], (D, FF), jnp.float32) * s, 'w2': jax.random.normal(ks[6], (FF, D), jnp.float32) * s, 'w3': jax.random.normal(ks[7], (D, FF), jnp.float32) * s, 'attn_norm_w': jnp.ones((D,), jnp.float32), 'ff_norm_w': jnp.ones((D,), jnp.float32), 'moe_norm_w': jnp.ones((D,), jnp.float32), 'router_w': jax.random.normal(ks[8], (D, E), jnp.float32) * s, 'ew1': jax.random.normal(ks[9], (E, D, EH), jnp.float32) * s, 'ew2': jax.random.normal(ks[10], (E, EH, D), jnp.float32) * s, 'ew3': jax.random.normal(ks[11], (E, D, EH), jnp.float32) * s}
    _L1_ffn_in = _L1_ffn_setup()

    def _L2_attn_setup():
        import jax, jax.numpy as jnp
        import numpy as np
        B, N, E, H = (2, 256, 128, 8)
        HID = 128
        D = HID // H
        EPS = 1e-08

        def rms_norm(x, scale):
            rms = jnp.linalg.norm(x, axis=-1, keepdims=True) * x.shape[-1] ** (-0.5)
            return scale * (x / (rms + EPS))
        key = jax.random.key(seed)
        ks = jax.random.split(key, 12)
        s = 0.02
        return {'x': jax.random.normal(ks[0], (B, N, E), jnp.float32), 'Wq': jax.random.normal(ks[1], (HID, E), jnp.float32) * s, 'bq': jnp.zeros((HID,), jnp.float32), 'Wk': jax.random.normal(ks[2], (HID, E), jnp.float32) * s, 'bk': jnp.zeros((HID,), jnp.float32), 'Wv': jax.random.normal(ks[3], (HID, E), jnp.float32) * s, 'bv': jnp.zeros((HID,), jnp.float32), 'Wu': jax.random.normal(ks[4], (HID, E), jnp.float32) * s, 'bu': jnp.zeros((HID,), jnp.float32), 'Wo': jax.random.normal(ks[5], (E, HID), jnp.float32) * s, 'bo': jnp.zeros((E,), jnp.float32), 'scale': jnp.ones((HID,), jnp.float32)}
    _L2_attn_in = _L2_attn_setup()

    def _L2_ffn_setup():
        import jax, jax.numpy as jnp
        import numpy as np
        B, S, D, H, E, K = (2, 128, 128, 64, 16, 4)
        HS = 2 * H

        def silu(z):
            return z * jax.nn.sigmoid(z)
        key = jax.random.key(seed)
        ks = jax.random.split(key, 8)
        sc = lambda fan_in: 1.0 / np.sqrt(fan_in)
        x = jax.random.normal(ks[0], (B, S, D), jnp.float32)
        gate_w = jax.random.normal(ks[1], (E, D), jnp.float32) * sc(D)
        ws_in = jax.random.normal(ks[2], (D, HS), jnp.float32) * sc(D)
        vs_in = jax.random.normal(ks[3], (D, HS), jnp.float32) * sc(D)
        ws_out = jax.random.normal(ks[4], (HS, D), jnp.float32) * sc(HS)
        e_win = jax.random.normal(ks[5], (E, D, H), jnp.float32) * sc(D)
        e_vin = jax.random.normal(ks[6], (E, D, H), jnp.float32) * sc(D)
        e_wout = jax.random.normal(ks[7], (E, H, D), jnp.float32) * sc(H)
        return {'x': x, 'gate_w': gate_w, 'ws_in': ws_in, 'vs_in': vs_in, 'ws_out': ws_out, 'e_win': e_win, 'e_vin': e_vin, 'e_wout': e_wout}
    _L2_ffn_in = _L2_ffn_setup()

    def _L3_attn_setup():
        import jax, jax.numpy as jnp
        import numpy as np
        E = 128
        H = 16
        D = E // H

        def _mha(x, Wq, bq, Wk, bk, Wv, bv, Wo, bo):
            q = jnp.einsum('bse,hde->bhsd', x, Wq) + bq[None, :, None, :]
            k = jnp.einsum('bse,hde->bhsd', x, Wk) + bk[None, :, None, :]
            v = jnp.einsum('bse,hde->bhsd', x, Wv) + bv[None, :, None, :]
            scores = jnp.einsum('bhsd,bhtd->bhst', q, k) / jnp.sqrt(jnp.asarray(D, x.dtype))
            w = jax.nn.softmax(scores, axis=-1)
            o = jnp.einsum('bhst,bhtd->bhsd', w, v)
            B, _, S, _ = o.shape
            o = jnp.transpose(o, (0, 2, 1, 3)).reshape(B, S, H * D)
            return o @ Wo.T + bo
        key = jax.random.key(seed)
        ks = jax.random.split(key, 9)
        s = 0.02
        return {'hidden_state': jax.random.normal(ks[0], (4, 128, E), jnp.float32), 'Wq': jax.random.normal(ks[1], (H, D, E), jnp.float32) * s, 'bq': jax.random.normal(ks[2], (H, D), jnp.float32) * s, 'Wk': jax.random.normal(ks[3], (H, D, E), jnp.float32) * s, 'bk': jax.random.normal(ks[4], (H, D), jnp.float32) * s, 'Wv': jax.random.normal(ks[5], (H, D, E), jnp.float32) * s, 'bv': jax.random.normal(ks[6], (H, D), jnp.float32) * s, 'Wo': jax.random.normal(ks[7], (E, E), jnp.float32) * s, 'bo': jax.random.normal(ks[8], (E,), jnp.float32) * s}
    _L3_attn_in = _L3_attn_setup()

    def _L3_ffn_setup():
        import jax, jax.numpy as jnp
        import numpy as np
        DIM = 128
        N_EXPERTS = 8
        D_FF = 256
        TOP_K = 2
        key = jax.random.key(seed)
        ks = jax.random.split(key, 5)
        s = 0.02
        return {'x': jax.random.normal(ks[0], (2, 256, DIM), dtype=jnp.float32), 'gate_w': jax.random.normal(ks[1], (N_EXPERTS, DIM), dtype=jnp.float32) * s, 'w1': jax.random.normal(ks[2], (N_EXPERTS, D_FF, DIM), dtype=jnp.float32) * s, 'w2': jax.random.normal(ks[3], (N_EXPERTS, DIM, D_FF), dtype=jnp.float32) * s, 'w3': jax.random.normal(ks[4], (N_EXPERTS, D_FF, DIM), dtype=jnp.float32) * s}
    _L3_ffn_in = _L3_ffn_setup()
    _d = {'L0_attn_X': _L0_attn_in['X'], 'L0_attn_W_in': _L0_attn_in['W_in'], 'L0_attn_W_out': _L0_attn_in['W_out'], 'L0_attn_ln_g': _L0_attn_in['ln_g'], 'L0_attn_ln_b': _L0_attn_in['ln_b'], 'L0_ffn_gate_w': _L0_ffn_in['gate_w'], 'L0_ffn_gate_b': _L0_ffn_in['gate_b'], 'L0_ffn_expert_w': _L0_ffn_in['expert_w'], 'L0_ffn_expert_b': _L0_ffn_in['expert_b'], 'L1_attn_wq': _L1_attn_in['wq'], 'L1_attn_bq': _L1_attn_in['bq'], 'L1_attn_wu': _L1_attn_in['wu'], 'L1_attn_bu': _L1_attn_in['bu'], 'L1_ffn_wq': _L1_ffn_in['wq'], 'L1_ffn_wk': _L1_ffn_in['wk'], 'L1_ffn_wv': _L1_ffn_in['wv'], 'L1_ffn_wo': _L1_ffn_in['wo'], 'L1_ffn_w1': _L1_ffn_in['w1'], 'L1_ffn_w2': _L1_ffn_in['w2'], 'L1_ffn_w3': _L1_ffn_in['w3'], 'L1_ffn_attn_norm_w': _L1_ffn_in['attn_norm_w'], 'L1_ffn_ff_norm_w': _L1_ffn_in['ff_norm_w'], 'L1_ffn_moe_norm_w': _L1_ffn_in['moe_norm_w'], 'L1_ffn_router_w': _L1_ffn_in['router_w'], 'L1_ffn_ew1': _L1_ffn_in['ew1'], 'L1_ffn_ew2': _L1_ffn_in['ew2'], 'L1_ffn_ew3': _L1_ffn_in['ew3'], 'L2_attn_Wq': _L2_attn_in['Wq'], 'L2_attn_bq': _L2_attn_in['bq'], 'L2_attn_Wk': _L2_attn_in['Wk'], 'L2_attn_bk': _L2_attn_in['bk'], 'L2_attn_Wv': _L2_attn_in['Wv'], 'L2_attn_bv': _L2_attn_in['bv'], 'L2_attn_Wu': _L2_attn_in['Wu'], 'L2_attn_bu': _L2_attn_in['bu'], 'L2_attn_Wo': _L2_attn_in['Wo'], 'L2_attn_bo': _L2_attn_in['bo'], 'L2_attn_scale': _L2_attn_in['scale'], 'L2_ffn_gate_w': _L2_ffn_in['gate_w'], 'L2_ffn_ws_in': _L2_ffn_in['ws_in'], 'L2_ffn_vs_in': _L2_ffn_in['vs_in'], 'L2_ffn_ws_out': _L2_ffn_in['ws_out'], 'L2_ffn_e_win': _L2_ffn_in['e_win'], 'L2_ffn_e_vin': _L2_ffn_in['e_vin'], 'L2_ffn_e_wout': _L2_ffn_in['e_wout'], 'L3_attn_Wq': _L3_attn_in['Wq'], 'L3_attn_bq': _L3_attn_in['bq'], 'L3_attn_Wk': _L3_attn_in['Wk'], 'L3_attn_bk': _L3_attn_in['bk'], 'L3_attn_Wv': _L3_attn_in['Wv'], 'L3_attn_bv': _L3_attn_in['bv'], 'L3_attn_Wo': _L3_attn_in['Wo'], 'L3_attn_bo': _L3_attn_in['bo'], 'L3_ffn_gate_w': _L3_ffn_in['gate_w'], 'L3_ffn_w1': _L3_ffn_in['w1'], 'L3_ffn_w2': _L3_ffn_in['w2'], 'L3_ffn_w3': _L3_ffn_in['w3']}
    _x0 = _d['L0_attn_X']
    _d['L0_attn_X'] = jax.random.normal(jax.random.fold_in(jax.random.key(seed), 1), (8, 512, 128), dtype=_x0.dtype)
    del _x0
    return _d

def reference(L0_attn_X, L0_attn_W_in, L0_attn_W_out, L0_attn_ln_g, L0_attn_ln_b, L0_ffn_gate_w, L0_ffn_gate_b, L0_ffn_expert_w, L0_ffn_expert_b, L1_attn_wq, L1_attn_bq, L1_attn_wu, L1_attn_bu, L1_ffn_wq, L1_ffn_wk, L1_ffn_wv, L1_ffn_wo, L1_ffn_w1, L1_ffn_w2, L1_ffn_w3, L1_ffn_attn_norm_w, L1_ffn_ff_norm_w, L1_ffn_moe_norm_w, L1_ffn_router_w, L1_ffn_ew1, L1_ffn_ew2, L1_ffn_ew3, L2_attn_Wq, L2_attn_bq, L2_attn_Wk, L2_attn_bk, L2_attn_Wv, L2_attn_bv, L2_attn_Wu, L2_attn_bu, L2_attn_Wo, L2_attn_bo, L2_attn_scale, L2_ffn_gate_w, L2_ffn_ws_in, L2_ffn_vs_in, L2_ffn_ws_out, L2_ffn_e_win, L2_ffn_e_vin, L2_ffn_e_wout, L3_attn_Wq, L3_attn_bq, L3_attn_Wk, L3_attn_bk, L3_attn_Wv, L3_attn_bv, L3_attn_Wo, L3_attn_bo, L3_ffn_gate_w, L3_ffn_w1, L3_ffn_w2, L3_ffn_w3):

    def _L0_attn_ref(X, W_in, W_out, ln_g, ln_b):
        import jax, jax.numpy as jnp
        import numpy as np
        D = 128
        ROT = D // 2
        B, S = (4, 1024)

        def _l2norm(x, eps=1e-06):
            return x * jax.lax.rsqrt(jnp.sum(x * x, axis=-1, keepdims=True) + eps)

        def _rotary(x, rot_dim):
            seq = x.shape[-2]
            half = rot_dim // 2
            inv_freq = 1.0 / 10000.0 ** (jnp.arange(0, rot_dim, 2, dtype=jnp.float32) / rot_dim)
            freqs = jnp.arange(seq, dtype=jnp.float32)[:, None] * inv_freq[None, :]
            freqs = jnp.repeat(freqs, 2, axis=-1)
            cos, sin = (jnp.cos(freqs), jnp.sin(freqs))
            xr, xp = (x[..., :rot_dim], x[..., rot_dim:])
            x2 = xr.reshape(*xr.shape[:-1], half, 2)
            rh = jnp.stack([-x2[..., 1], x2[..., 0]], axis=-1).reshape(xr.shape)
            return jnp.concatenate([xr * cos + rh * sin, xp], axis=-1)

        def _layernorm(x, g, b, eps=1e-05):
            mu = jnp.mean(x, axis=-1, keepdims=True)
            var = jnp.mean(jnp.square(x - mu), axis=-1, keepdims=True)
            return (x - mu) * jax.lax.rsqrt(var + eps) * g + b
        Xn = _layernorm(X, ln_g, ln_b)
        QKV = jnp.einsum('bsd,ed->bse', Xn, W_in)
        Q, K, V = jnp.split(QKV, 3, axis=-1)
        Q = _rotary(Q, ROT)
        K = _rotary(K, ROT)
        A = jnp.sum(_l2norm(K) * V, axis=-2)
        Y = A[:, None, :] * _l2norm(Q)
        Y = jnp.einsum('bsd,ed->bse', Y, W_out)
        return Y + X

    def _L0_ffn_ref(x, gate_w, gate_b, expert_w, expert_b):
        import jax, jax.numpy as jnp
        import numpy as np
        NUM_EXPERTS = 8
        D_MODEL = 128
        D_OUT = 128
        orig_shape = x.shape
        xt = x.reshape(-1, D_MODEL)
        logits = xt @ gate_w + gate_b
        gates = jax.nn.softmax(logits, axis=-1)
        sel = jnp.argmax(gates, axis=-1)
        onehot = jax.nn.one_hot(sel, NUM_EXPERTS, dtype=xt.dtype)
        y_all = jnp.einsum('td,edh->eth', xt, expert_w) + expert_b[:, None, :]
        out = jnp.einsum('te,eth->th', onehot, y_all)
        return out.reshape(*orig_shape[:-1], D_OUT)

    def _L1_attn_ref(x, wq, bq, wu, bu):
        import jax, jax.numpy as jnp
        import numpy as np
        import math
        EMB = 128
        HEADS = 16
        B, S = (2, 256)
        b, s, emb = x.shape
        hd = emb // HEADS
        q = jnp.einsum('bse,oe->bso', x, wq) + bq
        qh = q.reshape(HEADS, b, s, hd)
        kh = qh
        vh = qh
        scale = 1.0 / math.sqrt(emb)
        scores = jnp.einsum('hbqd,hbkd->hbqk', qh, kh) * scale
        attn = jax.nn.softmax(scores, axis=-1)
        out = jnp.einsum('hbqk,hbkd->hbqd', attn, vh)
        out = out.reshape(b, s, emb)
        return jnp.einsum('bse,oe->bso', out, wu) + bu

    def _L1_ffn_ref(x, wq, wk, wv, wo, w1, w2, w3, attn_norm_w, ff_norm_w, moe_norm_w, router_w, ew1, ew2, ew3):
        import jax, jax.numpy as jnp
        import numpy as np
        D = 128
        H = 16
        FF = 512
        E = 8
        K = 2
        EH = 128
        B, S = (2, 256)
        EPS = 1e-05

        def rmsnorm(x, w):
            v = jnp.mean(jnp.square(x), axis=-1, keepdims=True)
            return x * jax.lax.rsqrt(v + EPS) * w

        def _dense_path(x, wq, wk, wv, wo, w1, w2, w3, attn_norm_w, ff_norm_w):
            b, s, d = x.shape
            hd = d // H
            q = (x @ wq).reshape(b, s, H, hd)
            k = (x @ wk).reshape(b, s, H, hd)
            v = (x @ wv).reshape(b, s, H, hd)
            scores = jnp.einsum('bqhd,bkhd->bhqk', q, k) / np.sqrt(hd).astype(np.float32)
            causal = jnp.tril(jnp.ones((s, s), bool))
            scores = jnp.where(causal, scores, jnp.finfo(scores.dtype).min)
            attn = jax.nn.softmax(scores, axis=-1)
            o = jnp.einsum('bhqk,bkhd->bqhd', attn, v).reshape(b, s, d)
            h = x + rmsnorm(o @ wo, attn_norm_w)
            ffn = jax.nn.silu(h @ w1) * (h @ w3) @ w2
            return h + rmsnorm(ffn, ff_norm_w)

        def _sparse_path(x, router_w, ew1, ew2, ew3, moe_norm_w):
            b, s, d = x.shape
            xt = x.reshape(-1, d)
            probs = jax.nn.softmax(xt @ router_w, axis=-1)
            topw, topi = jax.lax.top_k(probs, K)
            g = jax.nn.silu(jnp.einsum('td,edh->eth', xt, ew1)) * jnp.einsum('td,edh->eth', xt, ew3)
            eo = jnp.einsum('eth,ehd->ted', g, ew2)
            sel = jnp.take_along_axis(eo, topi[:, :, None], axis=1)
            moe_out = jnp.sum(topw[:, :, None] * sel, axis=1).reshape(b, s, d)
            return rmsnorm(moe_out, moe_norm_w)
        dense_out = _dense_path(x, wq, wk, wv, wo, w1, w2, w3, attn_norm_w, ff_norm_w)
        sparse_out = _sparse_path(x, router_w, ew1, ew2, ew3, moe_norm_w)
        return dense_out + sparse_out

    def _L2_attn_ref(x, Wq, bq, Wk, bk, Wv, bv, Wu, bu, Wo, bo, scale):
        import jax, jax.numpy as jnp
        import numpy as np
        B, N, E, H = (2, 256, 128, 8)
        HID = 128
        D = HID // H
        EPS = 1e-08

        def rms_norm(x, scale):
            rms = jnp.linalg.norm(x, axis=-1, keepdims=True) * x.shape[-1] ** (-0.5)
            return scale * (x / (rms + EPS))
        n = x.shape[-2]
        q = x @ Wq.T + bq
        u = x @ Wu.T + bu
        k = x @ Wk.T + bk
        v = x @ Wv.T + bv
        u = jax.nn.silu(u)
        v = jax.nn.silu(v)
        to_heads = lambda t: t.reshape(*t.shape[:-1], H, D).swapaxes(-3, -2)
        q, k, v = map(to_heads, (q, k, v))
        q = jax.nn.elu(q)
        k = jax.nn.elu(k)
        mask = jnp.tril(jnp.ones((n, n), q.dtype))
        energy = jnp.einsum('bhnd,bhmd->bhnm', q, k) * mask
        out = jnp.einsum('bhnm,bhmd->bhnd', energy, v)
        out = out.swapaxes(-3, -2).reshape(*x.shape[:-1], HID)
        out = rms_norm(out, scale)
        out = u * out
        return out @ Wo.T + bo

    def _L2_ffn_ref(x, gate_w, ws_in, vs_in, ws_out, e_win, e_vin, e_wout):
        import jax, jax.numpy as jnp
        import numpy as np
        B, S, D, H, E, K = (2, 128, 128, 64, 16, 4)
        HS = 2 * H

        def silu(z):
            return z * jax.nn.sigmoid(z)
        b, s, d = x.shape
        T = b * s
        xf = x.reshape(T, d)
        g = jax.nn.sigmoid(xf @ gate_w.T)
        topv, topi = jax.lax.top_k(g, K)
        wn = topv / jnp.sum(topv, axis=-1, keepdims=True)
        combine = jnp.zeros_like(g).at[jnp.arange(T)[:, None], topi].add(wn)
        hin = jnp.einsum('td,edh->eth', xf, e_win)
        vin = jnp.einsum('td,edh->eth', xf, e_vin)
        h = silu(hin) * vin * combine.T[:, :, None]
        routed = jnp.einsum('eth,ehd->td', h, e_wout)
        shared = silu(xf @ ws_in) * (xf @ vs_in) @ ws_out
        return (shared + routed).reshape(b, s, d)

    def _L3_attn_ref(hidden_state, Wq, bq, Wk, bk, Wv, bv, Wo, bo):
        import jax, jax.numpy as jnp
        import numpy as np
        E = 128
        H = 16
        D = E // H

        def _mha(x, Wq, bq, Wk, bk, Wv, bv, Wo, bo):
            q = jnp.einsum('bse,hde->bhsd', x, Wq) + bq[None, :, None, :]
            k = jnp.einsum('bse,hde->bhsd', x, Wk) + bk[None, :, None, :]
            v = jnp.einsum('bse,hde->bhsd', x, Wv) + bv[None, :, None, :]
            scores = jnp.einsum('bhsd,bhtd->bhst', q, k) / jnp.sqrt(jnp.asarray(D, x.dtype))
            w = jax.nn.softmax(scores, axis=-1)
            o = jnp.einsum('bhst,bhtd->bhsd', w, v)
            B, _, S, _ = o.shape
            o = jnp.transpose(o, (0, 2, 1, 3)).reshape(B, S, H * D)
            return o @ Wo.T + bo
        return _mha(hidden_state, Wq, bq, Wk, bk, Wv, bv, Wo, bo)

    def _L3_ffn_ref(x, gate_w, w1, w2, w3):
        import jax, jax.numpy as jnp
        import numpy as np
        DIM = 128
        N_EXPERTS = 8
        D_FF = 256
        TOP_K = 2
        orig_shape = x.shape
        xf = x.reshape(-1, orig_shape[-1])
        scores = jnp.einsum('td,ed->te', xf, gate_w)
        probs = jax.nn.softmax(scores.astype(jnp.float32), axis=-1)
        weights, idx = jax.lax.top_k(probs, TOP_K)
        weights = weights / jnp.sum(weights, axis=-1, keepdims=True)
        weights = weights.astype(x.dtype)
        x1 = jax.nn.silu(jnp.einsum('td,efd->tef', xf, w1))
        x3 = jnp.einsum('td,efd->tef', xf, w3)
        out_all = jnp.einsum('tef,edf->ted', x1 * x3, w2)
        expert_outs = jnp.take_along_axis(out_all, idx[:, :, None], axis=1)
        result = jnp.einsum('tkd,tk->td', expert_outs, weights)
        return result.reshape(orig_shape)
    x = L0_attn_X
    x = x + _L0_attn_ref(_layernorm(x, axis=-1), L0_attn_W_in, L0_attn_W_out, L0_attn_ln_g, L0_attn_ln_b)
    x = x + _L0_ffn_ref(_layernorm(x, axis=-1), L0_ffn_gate_w, L0_ffn_gate_b, L0_ffn_expert_w, L0_ffn_expert_b)
    x = x + _L1_attn_ref(_layernorm(x, axis=-1), L1_attn_wq, L1_attn_bq, L1_attn_wu, L1_attn_bu)
    x = x + _L1_ffn_ref(_layernorm(x, axis=-1), L1_ffn_wq, L1_ffn_wk, L1_ffn_wv, L1_ffn_wo, L1_ffn_w1, L1_ffn_w2, L1_ffn_w3, L1_ffn_attn_norm_w, L1_ffn_ff_norm_w, L1_ffn_moe_norm_w, L1_ffn_router_w, L1_ffn_ew1, L1_ffn_ew2, L1_ffn_ew3)
    x = x + _L2_attn_ref(_layernorm(x, axis=-1), L2_attn_Wq, L2_attn_bq, L2_attn_Wk, L2_attn_bk, L2_attn_Wv, L2_attn_bv, L2_attn_Wu, L2_attn_bu, L2_attn_Wo, L2_attn_bo, L2_attn_scale)
    x = x + _L2_ffn_ref(_layernorm(x, axis=-1), L2_ffn_gate_w, L2_ffn_ws_in, L2_ffn_vs_in, L2_ffn_ws_out, L2_ffn_e_win, L2_ffn_e_vin, L2_ffn_e_wout)
    x = x + _L3_attn_ref(_layernorm(x, axis=-1), L3_attn_Wq, L3_attn_bq, L3_attn_Wk, L3_attn_bk, L3_attn_Wv, L3_attn_bv, L3_attn_Wo, L3_attn_bo)
    x = x + _L3_ffn_ref(_layernorm(x, axis=-1), L3_ffn_gate_w, L3_ffn_w1, L3_ffn_w2, L3_ffn_w3)
    return x

_drawn_inputs = setup_inputs


def setup_inputs(seed=0):
    import zlib

    import numpy as np

    out = dict(_drawn_inputs(seed))
    spreads = {'L0_attn_ln_g': (1.0, 0.2),
     'L0_attn_ln_b': (0.0, 0.1),
     'L0_ffn_gate_b': (0.0, 0.1),
     'L0_ffn_expert_b': (0.0, 0.1),
     'L1_ffn_attn_norm_w': (1.0, 0.2),
     'L1_ffn_ff_norm_w': (1.0, 0.2),
     'L1_ffn_moe_norm_w': (1.0, 0.6),
     'L2_attn_bq': (0.0, 0.8),
     'L2_attn_bk': (0.0, 0.761),
     'L2_attn_bv': (0.0, 0.791),
     'L2_attn_bu': (0.0, 0.8),
     'L2_attn_bo': (0.0, 0.1),
     'L2_attn_scale': (1.0, 0.6)}
    factors = {'L2_attn_Wq': 5.015,
     'L2_attn_Wk': 6.515,
     'L2_attn_Wv': 6.418,
     'L2_attn_Wu': 5.17,
     'L2_attn_Wo': 4.748,
     'L3_attn_Wq': 8.0,
     'L3_attn_bq': 8.0,
     'L3_attn_Wk': 8.0,
     'L3_attn_bk': 8.0,
     'L3_attn_Wv': 8.0,
     'L3_attn_bv': 8.0,
     'L3_attn_Wo': 8.0,
     'L3_attn_bo': 8.0,
     'L3_ffn_gate_w': 8.0,
     'L3_ffn_w1': 8.0,
     'L3_ffn_w2': 8.0,
     'L3_ffn_w3': 8.0}
    for name, (base, spread) in spreads.items():
        noise = np.random.default_rng([zlib.crc32(name.encode()), seed]).standard_normal(out[name].shape)
        drawn = base * np.exp(spread * noise) if base else spread * noise
        out[name] = jnp.asarray(drawn.astype(out[name].dtype))
    for name, factor in factors.items():
        out[name] = (out[name] * factor).astype(out[name].dtype)
    return out
```

```python
from contextlib import ExitStack

import concourse.bass as bass
from concourse import mybir
import numpy as np

F32 = mybir.dt.float32
BF16 = mybir.dt.bfloat16
ALU = mybir.AluOpType
ACT = mybir.ActivationFunctionType
AX_X = mybir.AxisListType.X

P = 128
NB = 8
S = 512
NT = S // P
UNITS = 16
HD = 8
GROUPS = UNITS // 4
ROT = P // 2
STACK = 6 * HD
ROWS = STACK + 2
NEG = -1.0e30

CONSTS = {}
_at = 0
for _name, _width in (("mean", P), ("ones", P), ("ident", P), ("rot", P), ("cos", S), ("sin", S), ("block", P),
                      ("head", 8), ("den", P), ("tril", S), ("tri8", 64), ("tri16", 256),
                      ("upper", P), ("lower", P), ("sel", 8 * P), ("pair", 8 * P)):
    CONSTS[_name] = (_at, _width)
    _at += _width
CONST_WIDTH = _at
RESIDENT = CONSTS["upper"][0]


def constant_table():
    c = {n: np.zeros((P, w), np.float32) for n, (_, w) in CONSTS.items()}
    i = np.arange(P)
    c["mean"][:] = 1.0 / P
    c["ones"][:] = 1.0
    c["ident"][i, i] = 1.0
    for a in range(0, ROT, 2):
        c["rot"][a + 1, a] = -1.0
        c["rot"][a, a + 1] = 1.0
    inv = (1.0 / np.float32(10000.0) ** (np.arange(0, ROT, 2, dtype=np.float32) / np.float32(ROT))).astype(np.float32)
    freqs = np.repeat(np.arange(S, dtype=np.float32)[:, None] * inv[None, :], 2, axis=-1)
    c["cos"][:] = 1.0
    c["cos"][:ROT] = np.cos(freqs).T
    c["sin"][:ROT] = np.sin(freqs).T
    c["block"][:] = (i[:, None] // 16) == (i[None, :] // 16)
    c["head"][:] = (i[:, None] // 16) == np.arange(8)[None, :]
    c["den"][:] = i[:, None] == (i[None, :] // 32) * 32 + HD
    c["tril"][:] = np.tile(i[:, None] <= i[None, :], (1, 4))
    for n, e in (("tri8", 8), ("tri16", 16)):
        c[n][:] = (np.arange(e)[None, :] < np.arange(e)[:, None]).reshape(1, e * e)
    c["upper"][:] = np.where(i[None, :] > i[:, None], NEG, 0.0)
    c["lower"][:] = np.where(i[None, :] < i[:, None], NEG, 0.0)
    sel = c["sel"].reshape(P, 8, P)
    pair = c["pair"].reshape(P, 8, P)
    for part in range(3):
        for e in range(8):
            sel[32 * part + e, e, :] = 1.0
            pair[32 * part + 2 * e, e, :64] = 1.0
            pair[32 * part + 2 * e + 1, e, 64:] = 1.0
    return np.concatenate([c[n] for n in CONSTS], axis=1)


EVENTS = dict(
    x_loaded=16, staged=576, stacked=576, mstaged=96, mstacked=48, ostaged=256, oback=16, x_stored=16, l2z=2,
    squared=15, act_step=46, rstd=15, copied=3, part1=5, prob=96, expd=3, silu=37, l2act=5, centred=9,
    normed=9, dve_step=137, rotated=2, y=5, resid=8, wtm=4, wsplit=4, masked=8, parts=5, vready=18, max1=192,
    msplit=3, osb=12, onorm=12, expin=2, gated=37, l2dve=5, statesb=3, emask=8, mean=9, var=13, qkv=3,
    turned=2, l2sum=2, yout=4, logits=4, wT=4, bcast=40, maskused=7, out0=1, proj=5, vtm=3, sc1=192, mT=3,
    sc2=96, pv=24, den=12, attn_out=1, gate=37, up=37, used=33, dense_out=1, moe1_out=1, l2a=5, state=3,
    energy=8, emused=7, l2out=1, moe2_out=1, moe3_out=1,
)


class Count:

    def __init__(self, sems, chain, turn=None):
        self.sems, self.chain, self.turn = sems, chain, turn
        self.seen, self.made, self.last = {}, {}, None

    def value(self, name, count):
        return count if self.turn is None else self.turn * EVENTS[name] + count

    def at(self, name, count):
        self.seen[name] = max(self.seen.get(name, 0), count)
        return self.value(name, count)

    def next(self, name, n=1):
        return self.at(name, self.seen.get(name, 0) + n)

    def tell(self, name=None, n=1):
        name = name or self.chain
        self.made[name] = self.made.get(name, 0) + n
        self.last = (name, self.made[name])
        return self.sems[name], n

    def own(self):
        name, count = self.last
        return self.sems[name], self.value(name, count)


def network(nc, inp, const, x_in, x_out):
    ctx = ExitStack()
    with ctx:
        def sb(name, shape, dt=F32):
            return ctx.enter_context(nc.sbuf_tensor(name, shape, dt))

        W = {}
        loads = []

        def weight(name, shape, src, dst=None):
            W[name] = sb("w_" + name, shape)
            loads.append(((dst or (lambda t: t[:]))(W[name]), src))

        cs = sb("cs", [P, RESIDENT])
        loads.append((cs[:], const[:, 0:RESIDENT]))
        C = {n: cs[:, a:a + w] for n, (a, w) in CONSTS.items() if a < RESIDENT}

        weight("in0", [P, 3 * P], inp["L0_attn_W_in"])
        weight("out0", [P, P], inp["L0_attn_W_out"])
        weight("gate0", [P, 8], inp["L0_ffn_gate_w"])
        weight("exp0", [P, 8, P], inp["L0_ffn_expert_w"].rearrange("e d h -> d e h"))
        weight("expb0", [8, P], inp["L0_ffn_expert_b"])
        weight("q1", [P, P], inp["L1_attn_wq"])
        weight("u1", [P, P], inp["L1_attn_wu"])
        for n in "qkv":
            weight(n + "f", [P, P], inp["L1_ffn_w" + n])
        weight("w1f", [P, 4 * P], inp["L1_ffn_w1"])
        weight("w3f", [P, 4 * P], inp["L1_ffn_w3"])
        weight("w2f", [P, 4, P], inp["L1_ffn_w2"].rearrange("(b p) d -> p b d", p=P))
        weight("routef", [P, 8], inp["L1_ffn_router_w"])
        weight("ew1f", [P, 8, P], inp["L1_ffn_ew1"].rearrange("e d h -> d e h"))
        weight("ew3f", [P, 8, P], inp["L1_ffn_ew3"].rearrange("e d h -> d e h"))
        weight("ew2f", [P, 8, P], inp["L1_ffn_ew2"].rearrange("e h d -> h e d"))
        for n in "qkvuo":
            weight(n + "2", [P, P], inp["L2_attn_W" + n])
        weight("gate2", [P, 16], inp["L2_ffn_gate_w"])
        weight("ws2", [P, P], inp["L2_ffn_ws_in"])
        weight("vs2", [P, P], inp["L2_ffn_vs_in"])
        weight("wso2", [P, P], inp["L2_ffn_ws_out"])
        weight("ewin2", [P, 16, 64], inp["L2_ffn_e_win"].rearrange("e d h -> d e h"))
        weight("evin2", [P, 16, 64], inp["L2_ffn_e_vin"].rearrange("e d h -> d e h"))
        weight("ewout2", [P, 8, P], inp["L2_ffn_e_wout"].rearrange("(p two) h d -> (two h) p d", two=2))
        for n in "qkv":
            weight(n + "3", [P, P], inp["L3_attn_W" + n])
        weight("gate3", [P, 8], inp["L3_ffn_gate_w"])
        weight("w13", [P, 8, 256], inp["L3_ffn_w1"])
        weight("w33", [P, 8, 256], inp["L3_ffn_w3"])
        weight("w23", [P, 2, 8, P], inp["L3_ffn_w2"].rearrange("(b p) e d -> p b e d", p=P))

        padded = {}
        for n, key in (("of", "L1_ffn_wo"), ("o3", "L3_attn_Wo")):
            padded[n] = sb("w_" + n, [P, GROUPS, P])
            src = inp[key].rearrange("(g c d) n -> c d g n", g=GROUPS, c=4)
            for c in range(4):
                loads.append((padded[n][32 * c:32 * c + HD, :, :], src[c]))

        VEC = ["L0_attn_ln_g", "L0_attn_ln_b", "L1_attn_bq", "L1_attn_bu", "L1_ffn_attn_norm_w", "L1_ffn_ff_norm_w",
               "L1_ffn_moe_norm_w", "L2_attn_bq", "L2_attn_bk", "L2_attn_bu", "L2_attn_bo", "L2_attn_scale",
               "L3_attn_bq", "L3_attn_bk", "L3_attn_bo"]
        vecs = sb("vecs", [P, len(VEC)])
        V = {}
        for i, n in enumerate(VEC):
            V[n] = vecs[:, i:i + 1]
            loads.append((V[n], inp[n].rearrange("(p one) -> p one", one=1)))
        ROWB = ["L1_attn_bq", "L2_attn_bk", "L2_attn_bv", "L3_attn_bv", "L0_ffn_gate_b"]
        rows = sb("rows", [1, len(ROWB), P])
        RB = {}
        for i, n in enumerate(ROWB):
            w = inp[n].shape[0]
            RB[n] = rows[0:1, i, 0:w]
            loads.append((RB[n], inp[n].rearrange("(one n) -> one n", one=1)))

        identb = sb("identb", [P, P], BF16)
        upperb = sb("upperb", [P, P], BF16)
        lowerb = sb("lowerb", [P, P], BF16)
        selb = sb("selb", [P, 8, P], BF16)
        pairb = sb("pairb", [P, 8, P], BF16)
        eps = sb("eps", [P, 2])
        EPS5, EPS6 = eps[:, 0:1], eps[:, 1:2]

        x = sb("x", [P, S])
        h = sb("h", [P, S])
        xc = sb("xc", [P, S])
        sq = sb("sq", [P, S])
        lnv = sb("lnv", [P, S])
        rs = sb("rs", [P, S])
        ta = sb("ta", [P, S])
        tb = sb("tb", [P, S])
        tc = sb("tc", [P, S])
        acc = sb("acc", [P, S])
        osum = sb("osum", [P, GROUPS, S])
        silu, gated = osum[:, 0:2, :], osum[:, 2:4, :]
        unit1 = sb("unit1", [P, 1])
        parts = sb("parts", [P, 2, 3, S], BF16)
        residue = sb("residue", [P, 2, S])
        Qs = sb("Qs", [P, UNITS, S], BF16)
        Ks = sb("Ks", [P, UNITS, S], BF16)
        Vp = sb("Vp", [P, NT, UNITS, 32])
        probs = sb("probs", [P, 8, 2, S])
        rec = rs
        mx = sb("mx", [P, NT, UNITS])
        msp = sb("msp", [64, 2, S], BF16)
        passing = probs[:, :, :, :].rearrange("p a b c -> p (a b c)")[:, 0:CONST_WIDTH - RESIDENT]
        loads.append((passing, const[:, RESIDENT:]))
        C.update({n: passing[:, a - RESIDENT:a - RESIDENT + w] for n, (a, w) in CONSTS.items() if a >= RESIDENT})
        lg = sb("lg", [P, NT, 16])
        pr = sb("pr", [P, NT, 16])
        cmp = silu.rearrange("p a b -> p (a b)")
        eqs = gated.rearrange("p a b -> p (a b)")
        rank = sb("rank", [P, NT, 16])
        red = sb("red", [P, NT])
        rinv = sb("rinv", [P, NT])
        wtm = sb("wtm", [P, NT, 16])
        wres = xc[0:16, :]
        wmid = tc[0:16, 0:S // 2].bitcast(BF16)
        wsp = sb("wsp", [96, S], BF16)
        Kh = Qs[:, :, :].rearrange("p a b -> p (a b)").bitcast(F32).rearrange("p (h s) -> p h s", h=8)
        Vz = Ks[:, :, :].rearrange("p a b -> p (a b)").bitcast(F32).rearrange("p (t h d) -> p t h d", t=NT, h=8)
        ktm = probs[:, 0, 0, :].rearrange("p (t d) -> p t d", t=NT)
        vtm = probs[:, 0, 1, :].rearrange("p (t d) -> p t d", t=NT)
        state = probs[:, 1, 0, :].rearrange("p (t d) -> p t d", t=NT)
        uu = probs[:, 1, 1, :]
        qe = probs[:, 2, 0, :]
        ke = probs[:, 2, 1, :]
        energy = probs[:, 3, :, :]
        em1 = probs[:, 4, 0, :]
        em2 = probs[:, 4, 1, :]
        em3 = probs[:, 5, 0, :]
        outT = probs[:, 6, 0, :]
        onehot = tb[0:16, :]

        E = ctx.enter_context(nc.psum_tensor("E", [P, 4, S], F32))
        M = ctx.enter_context(nc.psum_tensor("M", [P, 2, S], F32))
        O = ctx.enter_context(nc.psum_tensor("O", [P, 2, S], F32))
        Et, Mt = (lambda b: E[:, b, :]), (lambda b: M[:, b, :])
        MAXB = [M[:, 0, :], M[:, 1, :], O[:, 0, :], O[:, 1, :]]

        parts_dram = nc.dram_tensor("parts_dram", (2, 3, HD, UNITS, S), BF16).ap()
        minus_dram = nc.dram_tensor("minus_dram", (2, UNITS, S), BF16).ap()
        out_dram = nc.dram_tensor("out_dram", (P, S), F32).ap()

        names = ["w_loaded", "zeroed", "paced", "consts", "x_loaded", "x_stored",
                 "act_step", "dve_step", "pool_step",
                 "mean", "centred", "squared", "var", "rstd", "normed", "resid",
                 "qkv", "copied", "turned", "rotated", "l2sum", "y", "yout",
                 "logits", "expin", "expd", "wtm", "wT", "wsplit",
                 "gate", "up", "bcast", "silu", "gated", "used", "dense_out", "moe1_out", "moe2_out", "moe3_out", "attn_out", "out0",
                 "masked", "maskused",
                 "proj", "part1", "parts", "staged", "stacked", "vtm", "vready",
                 "sc1", "max1", "mT", "msplit", "mstaged", "mstacked", "sc2", "prob", "pv", "osb", "den", "onorm",
                 "ostaged", "oback",
                 "l2a", "l2act", "l2dve", "l2z", "state", "statesb", "energy", "emask", "emused", "l2out"]
        sems = {n: ctx.enter_context(nc.semaphore("s_" + n)) for n in names}
        n_loads = len(loads)
        totals = {}

        ATTN = {
            "chunk": dict(causal=False, chunk=True, scale=float(P) ** -0.5, q="q1", bq=V["L1_attn_bq"], k=None, bk=None,
                          v="q1", bv=RB["L1_attn_bq"]),
            "causal": dict(causal=True, chunk=False, scale=float(HD) ** -0.5, q="qf", bq=None, k="kf", bk=None,
                           v="vf", bv=None),
            "full": dict(causal=False, chunk=False, scale=float(HD) ** -0.5, q="q3", bq=V["L3_attn_bq"], k="k3",
                         bk=V["L3_attn_bk"], v="v3", bv=RB["L3_attn_bv"]),
        }

        def ffn_blocks(kind):
            if kind == "dense":
                return [(W["w1f"][:, P * b:P * b + P], W["w3f"][:, P * b:P * b + P], None, W["w2f"][:, b, :])
                        for b in range(4)]
            if kind == "moe1":
                return [(W["ew1f"][:, e, :], W["ew3f"][:, e, :], selb[0:96, e, :], W["ew2f"][:, e, :])
                        for e in range(8)]
            if kind == "moe2":
                pairs = [(W["ewin2"][:, 2 * e:2 * e + 2, :].rearrange("p a b -> p (a b)"),
                          W["evin2"][:, 2 * e:2 * e + 2, :].rearrange("p a b -> p (a b)"),
                          pairb[0:96, e, :], W["ewout2"][:, e, :]) for e in range(8)]
                return [(W["ws2"][:], W["vs2"][:], None, W["wso2"][:])] + pairs
            return [(W["w13"][:, e, P * b:P * b + P], W["w33"][:, e, P * b:P * b + P], selb[0:96, e, :],
                     W["w23"][:, b, e, :]) for e in range(8) for b in range(2)]

        def qcols(kt, causal):
            return slice(P * kt if causal else 0, S)

        def operand(stack, u, tile, n):
            return stack[0:n, u, :] if tile is None else stack[0:n, u, P * tile:P * tile + P]

        block = ctx.enter_context(nc.Block())

        @block.sync
        def _(sp_eng):
            for n, (dst, src) in enumerate(loads):
                if n == 1:
                    sp_eng.wait_ge(sems["zeroed"], 3)
                sp_eng.dma_start(dst, src).then_inc(sems["w_loaded"], 16)
            sp_eng.wait_ge(sems["consts"], 5)
            with sp_eng.Fori(0, NB) as b:
                sp = Count(sems, None, b)

                dma = sp_eng.dma_start

                def stack_up(cfg):
                    if cfg["chunk"]:
                        sp_eng.wait_ge(sems["parts"], sp.next("parts"))
                        for d in range(HD):
                            for a in range(3):
                                dma(parts_dram[0, a, d].rearrange("c (j t) -> j c t", t=32),
                                    parts[d:P:HD, 0, a, :].rearrange("j (c t) -> j c t", t=32)).then_inc(*sp.tell("staged", 16))
                        sp_eng.wait_ge(sems["staged"], sp.next("staged", 16 * 3 * HD))
                    else:
                        for side in range(2):
                            sp_eng.wait_ge(sems["parts"], sp.next("parts"))
                            for a in range(3):
                                dma(parts_dram[side, a].rearrange("d h s -> h d s"), parts[:, side, a, :]).then_inc(*sp.tell("staged", 16))
                        sp_eng.wait_ge(sems["staged"], sp.next("staged", 16 * 6))
                    src = [parts_dram[side] for side in range(2)]
                    k_side = src[0] if cfg["chunk"] else src[1]
                    for slot, (qp, kp) in enumerate(((0, 0), (0, 1), (1, 0), (0, 2), (2, 0), (1, 1))):
                        dma(Qs[HD * slot:HD * slot + HD, :, :], src[0][qp]).then_inc(*sp.tell("stacked", 16))
                        dma(Ks[HD * slot:HD * slot + HD, :, :], k_side[kp]).then_inc(*sp.tell("stacked", 16))
                    sp_eng.wait_ge(sems["msplit"], sp.next("msplit"))
                    for part in range(2):
                        if cfg["chunk"]:
                            dma(minus_dram[part].rearrange("c (q m) -> q c m", q=NT), msp[0:NT * UNITS, part, 0:P]).then_inc(*sp.tell("mstaged", 16))
                        else:
                            dma(minus_dram[part], msp[0:UNITS, part, :]).then_inc(*sp.tell("mstaged", 16))
                    sp_eng.wait_ge(sems["mstaged"], sp.next("mstaged", 32))
                    dma(Qs[STACK:ROWS, :, :], minus_dram).then_inc(*sp.tell("mstacked", 16))

                dma(x[:], x_in[b]).then_inc(*sp.tell("x_loaded", 16))
                stack_up(ATTN["chunk"])
                sp_eng.wait_ge(sems["onorm"], sp.next("onorm", GROUPS))
                for c in range(4):
                    for g in range(GROUPS):
                        tok = P * g + 32 * c
                        dma(out_dram[:, tok:tok + 32].rearrange("(j d) t -> d j t", d=HD),
                            osum[32 * c:32 * c + HD, g, :].rearrange("d (j t) -> d j t", t=32)).then_inc(*sp.tell("ostaged", 16))
                sp_eng.wait_ge(sems["ostaged"], sp.next("ostaged", 16 * 16))
                dma(outT, out_dram).then_inc(*sp.tell("oback", 16))
                stack_up(ATTN["causal"])
                sp_eng.wait_ge(sems["l2z"], sp.at("l2z", 2))
                sp_eng.sem_inc(sems["paced"], 1)
                stack_up(ATTN["full"])
                sp_eng.wait_ge(sems["resid"], sp.next("resid", 8))
                dma(x_out[b], x[:]).then_inc(*sp.tell("x_stored", 16))
                sp_eng.wait_ge(sems["x_stored"], sp.at("x_stored", 16))
                sp_eng.sem_inc(sems["paced"], 1)
            totals["sp"] = sp

        @block.gpsimd
        def _(pool_eng):
            pool0 = Count(sems, None)

            def fill(dst, value, name):
                pool_eng.memset(dst, value).then_inc(*pool0.tell(name))
                pool_eng.wait_ge(*pool0.own())

            for t in (padded["of"], padded["o3"], wsp):
                fill(t[:], 0.0, "zeroed")
            fill(eps[:, 0:1], 1e-5, "consts")
            fill(eps[:, 1:2], 1e-6, "consts")
            fill(Vp[:, :, :, HD:HD + 1], 1.0, "consts")
            fill(Vp[:, :, :, HD + 1:32], 0.0, "consts")
            fill(Ks[32:64, :, :], 1.0, "consts")
            with pool_eng.Fori(0, NB) as b:
                pool = Count(sems, "pool_step", b)
                pool_eng.wait_ge(sems["onorm"], pool.next("onorm", 2 * GROUPS))
                pool_eng.sem_inc(sems["paced"], 1)
                pool_eng.memset(Ks[:, :, :].rearrange("p a b -> p (a b)").bitcast(F32), 0.0).then_inc(*pool.tell("l2z"))
                pool_eng.wait_ge(sems["l2out"], pool.next("l2out"))
                pool_eng.sem_inc(sems["paced"], 1)
                pool_eng.memset(Ks[32:64, :, :], 1.0).then_inc(*pool.tell("l2z"))
                pool_eng.wait_ge(sems["x_stored"], pool.at("x_stored", 16))
            totals["pool"] = pool

        @block.scalar
        def _(act_eng):
            act_eng.wait_ge(sems["consts"], 5)
            act_eng.wait_ge(sems["w_loaded"], 16 * n_loads)
            with act_eng.Fori(0, NB) as b:
                act = Count(sems, "act_step", b)

                run = act_eng.activation

                def rsqrt(src, eps_ap):
                    run(lnv[:], src, ACT.Ln, bias=eps_ap).then_inc(*act.tell())
                    act_eng.wait_ge(*act.own())
                    run(rs[:], lnv[:], ACT.Exp, scale=-0.5).then_inc(*act.tell("rstd"))

                def layernorm():
                    act_eng.wait_ge(sems["centred"], act.next("centred"))
                    run(sq[:], xc[:], ACT.Square).then_inc(*act.tell("squared"))
                    act_eng.wait_ge(sems["var"], act.next("var"))
                    rsqrt(Et(0), EPS5)

                def softmax_exp(n):
                    act_eng.wait_ge(sems["expin"], act.next("expin"))
                    run(pr[:, :, 0:n], lg[:, :, 0:n], ACT.Exp).then_inc(*act.tell("expd"))

                def ffn(kind):
                    gated0 = act.seen.get("gated", 0)
                    for i in range(len(ffn_blocks(kind))):
                        act_eng.wait_ge(sems["gate"], act.next("gate"))
                        if i >= 2:
                            act_eng.wait_ge(sems["gated"], act.at("gated", gated0 + i - 1))
                        run(silu[:, i % 2, :], Et(i % 2), ACT.Silu).then_inc(*act.tell("silu"))
                    act.seen["gated"] = gated0 + len(ffn_blocks(kind))

                def attention(cfg):
                    sides = 1 if cfg["chunk"] else 2
                    for side in range(sides):
                        act_eng.wait_ge(sems["proj"], act.next("proj"))
                        bias = cfg["bq"] if side == 0 else cfg["bk"]
                        run(parts[:, side, 0, :], Et(side), ACT.Identity,
                            **({} if bias is None else {"bias": bias})).then_inc(*act.tell("part1"))
                    n0 = act.seen.get("pv", 0)
                    for n in range(2 * GROUPS):
                        if n >= 2:
                            act_eng.wait_ge(sems["pv"], act.at("pv", n0 + n - 1))
                        for c in range(4):
                            act_eng.wait_ge(sems["sc2"], act.next("sc2"))
                            slot, bank = 4 * (n % 2) + c, 2 * (c % 2)
                            if cfg["causal"]:
                                for kk in range(2):
                                    q = qcols(2 * (n % 2) + kk, True)
                                    run(probs[:, slot, kk, q], E[:, bank + kk, q], ACT.Exp, scale=cfg["scale"]).then_inc(*act.tell("prob" if kk else None))
                            else:
                                run(probs[:, slot], E[:, bank:bank + 2, :], ACT.Exp, scale=cfg["scale"]).then_inc(*act.tell("prob"))
                    act.seen["pv"] = n0 + 2 * GROUPS

                layernorm()
                layernorm()
                for i, dst in enumerate((ta, tb, tc)):
                    act_eng.wait_ge(sems["qkv"], act.next("qkv"))
                    run(dst[:], Et(i), ACT.Copy).then_inc(*act.tell("copied"))
                for i in range(2):
                    act_eng.wait_ge(sems["rotated"], act.next("rotated"))
                    run(sq[:] if i == 0 else lnv[:], (residue[:, i, :]), ACT.Square).then_inc(*act.tell("squared"))
                for i in range(2):
                    act_eng.wait_ge(sems["l2sum"], act.next("l2sum"))
                    run(silu[:, i, :], O[:, i, :], ACT.Ln, bias=EPS6).then_inc(*act.tell())
                    act_eng.wait_ge(*act.own())
                    run(silu[:, i, :], silu[:, i, :], ACT.Exp, scale=-0.5).then_inc(*act.tell("rstd"))
                layernorm()
                layernorm()
                attention(ATTN["chunk"])
                layernorm()
                attention(ATTN["causal"])
                act_eng.wait_ge(sems["attn_out"], act.next("attn_out"))
                run(sq[:], Et(0), ACT.Square).then_inc(*act.tell("squared"))
                act_eng.wait_ge(sems["var"], act.next("var"))
                rsqrt(Mt(0), EPS5)
                softmax_exp(8)
                for kind in ("dense", "moe1"):
                    ffn(kind)
                    act_eng.wait_ge(sems[kind + "_out"], act.next(kind + "_out"))
                    run(sq[:], O[:, 0, :], ACT.Square).then_inc(*act.tell("squared"))
                    act_eng.wait_ge(sems["var"], act.next("var"))
                    rsqrt(Mt(0), EPS5)
                layernorm()
                act_eng.wait_ge(sems["l2a"], act.next("l2a", 5))
                run(em1, Et(1), ACT.Exp, bias=V["L2_attn_bq"]).then_inc(*act.tell("l2act"))
                run(em2, Et(2), ACT.Exp, bias=V["L2_attn_bk"]).then_inc(*act.tell("l2act"))
                run(em3, Mt(1), ACT.Exp).then_inc(*act.tell("l2act"))
                run(uu, Et(0), ACT.Silu, bias=V["L2_attn_bu"]).then_inc(*act.tell("l2act"))
                run(probs[:, 0, 1, :], Mt(0), ACT.Silu).then_inc(*act.tell("l2act"))
                act_eng.wait_ge(sems["l2out"], act.next("l2out"))
                run(sq[:], O[:, 0, :], ACT.Square).then_inc(*act.tell("squared"))
                act_eng.wait_ge(sems["var"], act.next("var"))
                run(rs[:], Mt(0), ACT.Sqrt, scale=1.0).then_inc(*act.tell("rstd"))
                layernorm()
                act_eng.wait_ge(sems["logits"], act.at("logits", 3))
                run(pr[:, :, 0:16], M[:, 0, 0:64].rearrange("p (t e) -> p t e", t=NT), ACT.Sigmoid).then_inc(*act.tell("expd"))
                ffn("moe2")
                layernorm()
                attention(ATTN["full"])
                layernorm()
                softmax_exp(8)
                ffn("moe3")
                act_eng.wait_ge(sems["x_stored"], act.at("x_stored", 16))
            totals["act"] = act

        @block.vector
        def _(v):
            v.wait_ge(sems["w_loaded"], 16 * n_loads)
            v.wait_ge(sems["zeroed"], 3)
            v.wait_ge(sems["consts"], 5)
            for dst, n in ((identb, "ident"), (upperb, "upper"), (lowerb, "lower"),
                           (selb[:, :, :].rearrange("p a b -> p (a b)"), "sel"),
                           (pairb[:, :, :].rearrange("p a b -> p (a b)"), "pair")):
                v.tensor_copy(dst[:] if n in ("ident", "upper", "lower") else dst, C[n]).then_inc(sems["consts"], 1)
            with v.Fori(0, NB) as b:
                dve = Count(sems, "dve_step", b)

                tt, stt = v.tensor_tensor, v.scalar_tensor_tensor

                def ts(out, a, s1, s2, op0, op1):
                    return v.tensor_scalar(out, a, s1, None, op0) if op1 is None else \
                        v.tensor_scalar(out, a, s1, s2, op0, op1)

                def layernorm(src, dst, first=False, gain=None, bias=None):
                    if first:
                        v.wait_ge(sems["x_loaded"], dve.at("x_loaded", 16))
                    v.wait_ge(sems["mean"], dve.next("mean"))
                    tt(xc[:], src, Mt(0), ALU.subtract).then_inc(*dve.tell("centred"))
                    v.wait_ge(sems["rstd"], dve.next("rstd"))
                    if gain is None:
                        tt(dst, xc[:], rs[:], ALU.mult).then_inc(*dve.tell("normed"))
                    else:
                        tt(dst, xc[:], rs[:], ALU.mult).then_inc(*dve.tell())
                        v.wait_ge(*dve.own())
                        ts(dst, dst, gain, bias, ALU.mult, ALU.add).then_inc(*dve.tell("normed"))

                def top(n, k, src, name=None):
                    p = src[:, :, 0:n]
                    others = p.unsqueeze(2).broadcast_to([P, NT, n, n])
                    mine = p.unsqueeze(3).broadcast_to([P, NT, n, n])
                    tri = C[f"tri{n}"].rearrange("p (a b) -> p a b", a=n).unsqueeze(1).broadcast_to([P, NT, n, n])
                    cv = cmp[:, 0:NT * n * n] \
                        .rearrange("p (t a b) -> p t a b", t=NT, a=n)
                    ev = eqs[:, 0:NT * n * n] \
                        .rearrange("p (t a b) -> p t a b", t=NT, a=n)
                    tt(ev, others, mine, ALU.is_equal).then_inc(*dve.tell())
                    tt(cv, others, mine, ALU.is_gt).then_inc(*dve.tell())
                    v.wait_ge(*dve.own())
                    tt(ev, ev, tri, ALU.mult).then_inc(*dve.tell())
                    v.wait_ge(*dve.own())
                    tt(cv, cv, ev, ALU.add).then_inc(*dve.tell())
                    v.wait_ge(*dve.own())
                    v.tensor_reduce(rank[:, :, 0:n], cv, AX_X, ALU.add).then_inc(*dve.tell())
                    v.wait_ge(*dve.own())
                    stt(wtm[:, :, 0:n], rank[:, :, 0:n], float(k), p, ALU.is_lt, ALU.mult).then_inc(*dve.tell(name))
                    v.wait_ge(*dve.own())

                def softmax(n):
                    lp = M[:, 0, 0:NT * n].rearrange("p (t e) -> p t e", t=NT)
                    v.wait_ge(sems["logits"], dve.next("logits"))
                    v.tensor_reduce(red[:], lp, AX_X, ALU.max).then_inc(*dve.tell())
                    v.wait_ge(*dve.own())
                    tt(lg[:, :, 0:n], lp, red[:].unsqueeze(2).broadcast_to([P, NT, n]), ALU.subtract).then_inc(*dve.tell("expin"))
                    v.wait_ge(sems["expd"], dve.next("expd"))
                    total(n, pr)
                    tt(pr[:, :, 0:n], pr[:, :, 0:n], rinv[:].unsqueeze(2).broadcast_to([P, NT, n]), ALU.mult).then_inc(*dve.tell())
                    v.wait_ge(*dve.own())

                def total(n, src):
                    v.tensor_reduce(red[:], src[:, :, 0:n], AX_X, ALU.add).then_inc(*dve.tell())
                    v.wait_ge(*dve.own())
                    v.reciprocal(rinv[:], red[:]).then_inc(*dve.tell())
                    v.wait_ge(*dve.own())

                def scale_weights(n):
                    total(n, wtm)
                    tt(wtm[:, :, 0:n], wtm[:, :, 0:n], rinv[:].unsqueeze(2).broadcast_to([P, NT, n]), ALU.mult).then_inc(*dve.tell("wtm"))

                def split_weights(n):
                    v.wait_ge(sems["wT"], dve.next("wT"))
                    src = M[0:n, 1, :]
                    v.tensor_copy(wsp[0:n, :], src).then_inc(*dve.tell())
                    v.wait_ge(*dve.own())
                    tt(wres[0:n, :], src, wsp[0:n, :], ALU.subtract).then_inc(*dve.tell())
                    v.wait_ge(*dve.own())
                    v.tensor_copy(wmid[0:n, :], wres[0:n, :]).then_inc(*dve.tell())
                    v.wait_ge(*dve.own())
                    v.tensor_copy(wsp[32:32 + n, :], wmid[0:n, :]).then_inc(*dve.tell())
                    tt(wsp[64:64 + n, :], wres[0:n, :], wmid[0:n, :], ALU.subtract).then_inc(*dve.tell("wsplit"))

                def ffn(kind):
                    used0 = dve.seen.get("used", 0)
                    for i, (_, _, sel, _) in enumerate(ffn_blocks(kind)):
                        v.wait_ge(sems["silu"], dve.next("silu"))
                        s = silu[:, i % 2, :]
                        if sel is not None:
                            v.wait_ge(sems["bcast"], dve.next("bcast"))
                            tt(s, s, Et(2 + i % 2), ALU.mult).then_inc(*dve.tell())
                            v.wait_ge(*dve.own())
                        v.wait_ge(sems["up"], dve.next("up"))
                        if i >= 2:
                            v.wait_ge(sems["used"], dve.at("used", used0 + i - 1))
                        tt(gated[:, i % 2, :], s, Mt(i % 2), ALU.mult).then_inc(*dve.tell("gated"))
                    dve.seen["used"] = used0 + len(ffn_blocks(kind)) - 1

                def attention(cfg):
                    chunk, causal = cfg["chunk"], cfg["causal"]
                    sides = 1 if chunk else 2
                    for side in range(sides):
                        bias = cfg["bq"] if side == 0 else cfg["bk"]
                        v.wait_ge(sems["part1"], dve.next("part1"))
                        if bias is None:
                            tt(residue[:, side, :], Et(side), parts[:, side, 0, :], ALU.subtract).then_inc(*dve.tell())
                        else:
                            stt(residue[:, side, :], Et(side), bias, parts[:, side, 0, :], ALU.add, ALU.subtract).then_inc(*dve.tell())
                        v.wait_ge(*dve.own())
                        v.tensor_copy(parts[:, side, 1, :], residue[:, side, :]).then_inc(*dve.tell())
                        v.wait_ge(*dve.own())
                        tt(parts[:, side, 2, :], residue[:, side, :], parts[:, side, 1, :], ALU.subtract).then_inc(*dve.tell("parts"))
                    v.wait_ge(sems["vtm"], dve.next("vtm"))
                    if chunk:
                        vt = M[:, 0, :].rearrange("p (i k j d) -> p i k j d", i=NT, k=NT, j=4)
                        vd = Vp[:, :, :, :].rearrange("p k (i c) w -> p k i c w", c=4)
                        for c in range(4):
                            for j in range(4):
                                v.tensor_copy(
                                    vd[32 * j:32 * j + 32, :, :, c, 0:HD].rearrange("p k i d -> p i k d"),
                                    vt[32 * c:32 * c + 32, :, :, j, :]).then_inc(*dve.tell("vready"))
                    else:
                        v.tensor_copy(Vp[:, :, :, 0:HD], M[:, 0, :].rearrange("p (t h d) -> p t h d", t=NT, d=HD)).then_inc(*dve.tell("vready"))
                    for n in range(UNITS * NT):
                        u, qt = divmod(n, NT)
                        keys = P * (qt + 1) if causal else S
                        v.wait_ge(sems["sc1"], dve.next("sc1"))
                        v.tensor_reduce(mx[:, qt, u:u + 1], MAXB[n % 4][:, 0:keys], AX_X, ALU.max).then_inc(*dve.tell("max1"))
                    v.wait_ge(sems["mT"], dve.next("mT"))
                    r = slice(0, 64) if chunk else slice(0, UNITS)
                    cols = slice(0, P) if chunk else slice(0, S)
                    ts(msp[r, 0, cols], M[r, 0, cols], -1.0, None, ALU.mult, None).then_inc(*dve.tell())
                    v.wait_ge(*dve.own())
                    stt(msp[r, 1, cols], M[r, 0, cols], -1.0, msp[r, 0, cols], ALU.mult, ALU.subtract).then_inc(*dve.tell("msplit"))
                    pv0 = dve.seen.get("pv", 0)
                    for g in range(GROUPS):
                        v.wait_ge(sems["pv"], dve.at("pv", pv0 + 2 * g + 2))
                        v.tensor_copy(osum[:, g, :], O[:, g % 2, :]).then_inc(*dve.tell("osb"))
                        v.wait_ge(sems["den"], dve.next("den"))
                        v.reciprocal(rec[:], Mt(g % 2)).then_inc(*dve.tell())
                        v.wait_ge(*dve.own())
                        tt(osum[:, g, :], osum[:, g, :], rec[:], ALU.mult).then_inc(*dve.tell("onorm"))

                layernorm(x[:], h[:], first=True)
                layernorm(h[:], acc[:], gain=V["L0_attn_ln_g"], bias=V["L0_attn_ln_b"])
                for i, src in enumerate((ta, tb)):
                    v.wait_ge(sems["copied"], dve.next("copied"))
                    tt(gated[:, i, :], src[:], C["cos"], ALU.mult).then_inc(*dve.tell())
                    v.wait_ge(sems["turned"], dve.next("turned"))
                    tt(residue[:, i, :], Mt(i), C["sin"], ALU.mult).then_inc(*dve.tell())
                    v.wait_ge(*dve.own())
                    tt(residue[:, i, :], residue[:, i, :], gated[:, i, :], ALU.add).then_inc(*dve.tell("rotated"))
                v.wait_ge(sems["rstd"], dve.next("rstd", 2))
                tt(tb[:], residue[:, 1, :], silu[:, 1, :], ALU.mult).then_inc(*dve.tell())
                v.wait_ge(sems["copied"], dve.next("copied"))
                v.wait_ge(*dve.own())
                v.tensor_tensor_reduce(tb[:], tb[:], tc[:], 1.0, 0.0, ALU.mult, ALU.add, unit1[:]).then_inc(*dve.tell())
                v.wait_ge(*dve.own())
                stt(ta[:], residue[:, 0, :], unit1[:], silu[:, 0, :], ALU.mult, ALU.mult).then_inc(*dve.tell("y"))
                v.wait_ge(sems["yout"], dve.next("yout"))
                tt(ta[:], h[:], Et(0), ALU.add).then_inc(*dve.tell())
                v.wait_ge(*dve.own())
                tt(x[:], x[:], ta[:], ALU.add).then_inc(*dve.tell("resid"))

                layernorm(x[:], h[:])
                v.wait_ge(sems["logits"], dve.next("logits"))
                v.tensor_copy(lg[:, :, 0:8], M[:, 0, 0:32].rearrange("p (t e) -> p t e", t=NT)).then_inc(*dve.tell())
                v.wait_ge(*dve.own())
                top(8, 1, lg)
                ts(wtm[:, :, 0:8], rank[:, :, 0:8], 1.0, None, ALU.is_lt, None).then_inc(*dve.tell("wtm"))
                split_weights(8)
                v.wait_ge(*dve.own())
                v.tensor_copy(onehot[0:8, :], wsp[0:8, :]).then_inc(*dve.tell("y"))
                used0 = dve.seen.get("maskused", 0)
                for e in range(8):
                    v.wait_ge(sems["bcast"], dve.next("bcast"))
                    if e >= 2:
                        v.wait_ge(sems["maskused"], dve.at("maskused", used0 + e - 1))
                    tt(gated[:, e % 2, :], h[:], Et(e % 2), ALU.mult).then_inc(*dve.tell("masked"))
                v.wait_ge(sems["out0"], dve.next("out0"))
                tt(x[:], x[:], O[:, 0, :], ALU.add).then_inc(*dve.tell("resid"))

                layernorm(x[:], h[:])
                attention(ATTN["chunk"])
                v.wait_ge(sems["yout"], dve.next("yout"))
                stt(x[:], Et(0), V["L1_attn_bu"], x[:], ALU.add, ALU.add).then_inc(*dve.tell("resid"))

                layernorm(x[:], h[:])
                attention(ATTN["causal"])

                def rms_add(src, gain, dst, base, name):
                    v.wait_ge(sems["rstd"], dve.next("rstd"))
                    stt(ta[:], src, gain, rs[:], ALU.mult, ALU.mult).then_inc(*dve.tell())
                    v.wait_ge(*dve.own())
                    tt(dst, ta[:], base, ALU.add).then_inc(*dve.tell(name))

                rms_add(Et(0), V["L1_ffn_attn_norm_w"], acc[:], h[:], "y")
                softmax(8)
                top(8, 2, pr, "wtm")
                split_weights(8)
                ffn("dense")
                rms_add(O[:, 0, :], V["L1_ffn_ff_norm_w"], tb[:], acc[:], "y")
                ffn("moe1")
                rms_add(O[:, 0, :], V["L1_ffn_moe_norm_w"], tb[:], tb[:], None)
                v.wait_ge(*dve.own())
                tt(x[:], x[:], tb[:], ALU.add).then_inc(*dve.tell("resid"))

                layernorm(x[:], h[:])
                for i, (src, e, bias, dst) in enumerate(((Et(1), em1, V["L2_attn_bq"], qe), (Et(2), em2, V["L2_attn_bk"], ke),
                                                         (Mt(1), em3, None, probs[:, 0, 0, :]))):
                    v.wait_ge(sems["l2act"], dve.next("l2act"))
                    ts(e, e, 1.0, -1.0, ALU.min, ALU.add).then_inc(*dve.tell())
                    v.wait_ge(*dve.own())
                    if bias is None:
                        stt(dst, src, 0.0, e, ALU.max, ALU.add).then_inc(*dve.tell("l2dve"))
                    else:
                        ts(ta[:], src, bias, 0.0, ALU.add, ALU.max).then_inc(*dve.tell())
                        v.wait_ge(*dve.own())
                        tt(dst, ta[:], e, ALU.add).then_inc(*dve.tell("l2dve"))
                v.wait_ge(*dve.own())
                for hh in range(8):
                    ts(Kh[:, hh, :], ke, C["head"][:, hh:hh + 1], None, ALU.mult, None).then_inc(*dve.tell())
                v.wait_ge(sems["l2act"], dve.next("l2act", 2))
                v.wait_ge(sems["l2z"], dve.at("l2z", 1))
                flat = Vz.rearrange("p t h d -> p t (h d)")
                vh = vtm.rearrange("p t (h d) -> p t h d", d=16)
                v.tensor_copy(flat[:, :, 0:7 * 144].rearrange("p t (h w) -> p t h w", w=144)[:, :, :, 0:16],
                                       vh[:, :, 0:7, :]).then_inc(*dve.tell("l2dve"))
                v.tensor_copy(flat[:, :, 7 * 144:8 * P], vh[:, :, 7, :]).then_inc(*dve.tell("l2dve"))
                for j in range(NT - 1):
                    v.wait_ge(sems["state"], dve.next("state"))
                    tt(state[:, j, :], O[:, 1, 0:P], C["block"], ALU.mult).then_inc(*dve.tell("statesb"))
                em0 = dve.seen.get("emused", 0)
                for n in range(2 * NT):
                    v.wait_ge(sems["energy"], dve.next("energy"))
                    if n >= 2:
                        v.wait_ge(sems["emused"], dve.at("emused", em0 + n - 1))
                    tt(energy[:, n % 2, :], C["tril"], Et(n % 2), ALU.mult).then_inc(*dve.tell("emask"))
                v.wait_ge(sems["rstd"], dve.next("rstd"))
                ts(rs[:], rs[:], 1e-8, None, ALU.add, None).then_inc(*dve.tell())
                v.wait_ge(*dve.own())
                v.reciprocal(lnv[:], rs[:]).then_inc(*dve.tell())
                v.wait_ge(*dve.own())
                stt(ta[:], O[:, 0, :], V["L2_attn_scale"], lnv[:], ALU.mult, ALU.mult).then_inc(*dve.tell())
                v.wait_ge(*dve.own())
                tt(ta[:], ta[:], uu, ALU.mult).then_inc(*dve.tell("y"))
                v.wait_ge(sems["yout"], dve.next("yout"))
                stt(x[:], Et(0), V["L2_attn_bo"], x[:], ALU.add, ALU.add).then_inc(*dve.tell("resid"))

                layernorm(x[:], h[:])
                v.wait_ge(sems["logits"], dve.next("logits"))
                v.wait_ge(sems["expd"], dve.next("expd"))
                top(16, 4, pr)
                scale_weights(16)
                split_weights(16)
                ffn("moe2")
                v.wait_ge(sems["moe2_out"], dve.next("moe2_out"))
                tt(x[:], x[:], O[:, 0, :], ALU.add).then_inc(*dve.tell("resid"))

                layernorm(x[:], h[:])
                attention(ATTN["full"])
                v.wait_ge(sems["yout"], dve.next("yout"))
                stt(x[:], Et(0), V["L3_attn_bo"], x[:], ALU.add, ALU.add).then_inc(*dve.tell("resid"))
                layernorm(x[:], h[:])
                softmax(8)
                top(8, 2, pr)
                scale_weights(8)
                split_weights(8)
                ffn("moe3")
                v.wait_ge(sems["moe3_out"], dve.next("moe3_out"))
                tt(x[:], x[:], O[:, 0, :], ALU.add).then_inc(*dve.tell("resid"))
                v.wait_ge(sems["x_stored"], dve.at("x_stored", 16))
            totals["dve"] = dve

        @block.tensor
        def _(t_eng):
            t_eng.wait_ge(sems["w_loaded"], 16 * n_loads)
            t_eng.wait_ge(sems["consts"], 10)
            with t_eng.Fori(0, NB) as b:
                pe = Count(sems, None, b)

                def mm(out, lhsT, rhs, start=True, stop=True, **kw):
                    return t_eng.matmul(out, lhsT, rhs, start=start, stop=stop, **kw)

                def layernorm(src, ready, n=1):
                    t_eng.wait_ge(sems[ready], pe.next(ready, n))
                    mm(Mt(0), C["mean"], src).then_inc(*pe.tell("mean"))
                    t_eng.wait_ge(sems["squared"], pe.next("squared"))
                    mm(Et(0), C["mean"], sq[:]).then_inc(*pe.tell("var"))

                def route(n, weights, bias=None):
                    for t in range(NT):
                        out = M[:, 0, n * t:n * t + n]
                        ins = mm(out, h[:, P * t:P * t + P], weights,
                           stop=bias is None)
                        if bias is None and t == NT - 1:
                            ins.then_inc(*pe.tell("logits"))
                        if bias is not None:
                            ins = mm(out, C["ones"][0:1, :], bias, start=False)
                            if t == NT - 1:
                                ins.then_inc(*pe.tell("logits"))

                def turn_weights(n):
                    t_eng.wait_ge(sems["wtm"], pe.next("wtm"))
                    for t in range(NT):
                        ins = t_eng.transpose(M[0:n, 1, P * t:P * t + P], wtm[:, t, 0:n], C["ident"])
                    ins.then_inc(*pe.tell("wT"))

                def ffn(kind, rhs):
                    blocks = ffn_blocks(kind)
                    silu0, gated0 = pe.seen.get("silu", 0), pe.seen.get("gated", 0)
                    for i in range(len(blocks) + 1):
                        if i < len(blocks):
                            w1, w3, sel, _ = blocks[i]
                            if i >= 2:
                                t_eng.wait_ge(sems["silu"], pe.at("silu", silu0 + i - 1))
                            mm(Et(i % 2), w1, rhs).then_inc(*pe.tell("gate"))
                            if i >= 2:
                                t_eng.wait_ge(sems["gated"], pe.at("gated", gated0 + i - 1))
                            if sel is not None:
                                mm(Et(2 + i % 2), sel, wsp[:, :]).then_inc(*pe.tell("bcast"))
                            mm(Mt(i % 2), w3, rhs).then_inc(*pe.tell("up"))
                        if i >= 1:
                            t_eng.wait_ge(sems["gated"], pe.at("gated", gated0 + i))
                            mm(O[:, 0, :], blocks[i - 1][3], gated[:, (i - 1) % 2, :],
                               start=(i == 1), stop=(i == len(blocks))).then_inc(*pe.tell("used" if i < len(blocks) else kind + "_out"))
                    pe.seen["silu"] = silu0 + len(blocks)

                def attention(cfg):
                    chunk, causal = cfg["chunk"], cfg["causal"]
                    mm(Et(0), W[cfg["q"]][:], h[:]).then_inc(*pe.tell("proj"))
                    if not chunk:
                        mm(Et(1), W[cfg["k"]][:], h[:]).then_inc(*pe.tell("proj"))
                    for t in range(NT):
                        out = M[:, 0, P * t:P * t + P]
                        ins = mm(out, h[:, P * t:P * t + P], W[cfg["v"]][:],
                           stop=cfg["bv"] is None)
                        if cfg["bv"] is None and t == NT - 1:
                            ins.then_inc(*pe.tell("vtm"))
                        if cfg["bv"] is not None:
                            ins = mm(out, C["ones"][0:1, :], cfg["bv"], start=False)
                            if t == NT - 1:
                                ins.then_inc(*pe.tell("vtm"))
                    t_eng.wait_ge(sems["vready"], pe.next("vready", 16 if chunk else 1))
                    t_eng.wait_ge(sems["stacked"], pe.next("stacked", 16 * 12))
                    max0 = pe.seen.get("max1", 0)
                    for n in range(UNITS * NT):
                        u, qt = divmod(n, NT)
                        keys = P * (qt + 1) if causal else S
                        if n >= 4:
                            t_eng.wait_ge(sems["max1"], pe.at("max1", max0 + n - 3))
                        ins = mm(MAXB[n % 4][:, 0:keys], operand(Qs, u, qt, STACK), operand(Ks, u, None, STACK)[:, 0:keys], stop=not causal)
                        if not causal:
                            ins.then_inc(*pe.tell("sc1"))
                        if causal:
                            mm(MAXB[n % 4][:, keys - P:keys], identb[:], upperb[:], start=False).then_inc(*pe.tell("sc1"))
                    t_eng.wait_ge(sems["max1"], pe.at("max1", max0 + UNITS * NT))
                    t_eng.sem_inc(sems["paced"], 1)
                    if chunk:
                        ins = t_eng.transpose(M[0:64, 0, 0:P], mx[:, :, :].rearrange("p a b -> p (a b)"), C["ident"])
                    else:
                        for t in range(NT):
                            ins = t_eng.transpose(M[0:UNITS, 0, P * t:P * t + P], mx[:, t, :], C["ident"])
                    ins.then_inc(*pe.tell("mT"))
                    t_eng.wait_ge(sems["mstacked"], pe.next("mstacked", 16))
                    prob0 = pe.seen.get("prob", 0)
                    osb0 = pe.seen.get("osb", 0)
                    onorm0 = pe.seen.get("onorm", 0)
                    slots = 0

                    def sums(n):
                        g, half = divmod(n, 2)
                        t_eng.wait_ge(sems["prob"], pe.at("prob", prob0 + 4 * n + 4))
                        if half == 0 and g >= 2:
                            t_eng.wait_ge(sems["osb"], pe.at("osb", osb0 + g - 1))
                        for kk in range(2):
                            kt = 2 * half + kk
                            q = qcols(kt, causal)
                            for c in range(4):
                                ins = mm(O[32 * c:32 * c + 32, g % 2, q], Vp[:, kt, 4 * g + c, :],
                                   probs[:, 4 * (n % 2) + c, kk, q],
                                   start=kt == 0, stop=kt == NT - 1)
                                if kk == 1 and c == 3:
                                    ins.then_inc(*pe.tell("pv"))

                    def denominators(g):
                        t_eng.wait_ge(sems["osb"], pe.at("osb", osb0 + g + 1))
                        if g >= 2:
                            t_eng.wait_ge(sems["onorm"], pe.at("onorm", onorm0 + g - 1))
                        mm(Mt(g % 2), C["den"], osum[:, g, :]).then_inc(*pe.tell("den"))

                    for n in range(2 * GROUPS):
                        for c in range(4):
                            if slots >= 2:
                                t_eng.wait_ge(sems["prob"], pe.at("prob", prob0 + slots - 1))
                            slots += 1
                            u = 4 * (n // 2) + c
                            for kk in range(2):
                                kt = 2 * (n % 2) + kk
                                q = qcols(kt, causal)
                                ins = mm(E[:, 2 * (c % 2) + kk, q], operand(Ks, u, kt, ROWS),
                                   operand(Qs, u, None, ROWS)[:, q],
                                   stop=not causal)
                                if kk == 1 and not causal:
                                    ins.then_inc(*pe.tell("sc2"))
                                if causal:
                                    ins = mm(E[:, 2 * (c % 2) + kk, P * kt:P * kt + P], identb[:], lowerb[:], start=False)
                                    if kk == 1:
                                        ins.then_inc(*pe.tell("sc2"))
                        if n >= 1:
                            sums(n - 1)
                        if n >= 2 and n % 2 == 0:
                            denominators(n // 2 - 1)
                    sums(2 * GROUPS - 1)
                    denominators(GROUPS - 1)
                    t_eng.wait_ge(sems["onorm"], pe.at("onorm", onorm0 + GROUPS))

                def project(weights, name):
                    for g in range(GROUPS):
                        ins = mm(Et(0), weights[:, g, :], osum[:, g, :],
                           start=g == 0, stop=g == GROUPS - 1)
                        if g == GROUPS - 1:
                            ins.then_inc(*pe.tell(name))

                def rms():
                    t_eng.wait_ge(sems["squared"], pe.next("squared"))
                    mm(Mt(0), C["mean"], sq[:]).then_inc(*pe.tell("var"))

                layernorm(x[:], "x_loaded", 16)
                layernorm(h[:], "normed")
                t_eng.wait_ge(sems["normed"], pe.next("normed"))
                for i in range(3):
                    mm(Et(i), W["in0"][:, P * i:P * i + P], acc[:]).then_inc(*pe.tell("qkv"))
                for i, src in enumerate((ta, tb)):
                    t_eng.wait_ge(sems["copied"], pe.next("copied"))
                    mm(Mt(i), C["rot"], src[:]).then_inc(*pe.tell("turned"))
                for i, src in enumerate((sq, lnv)):
                    t_eng.wait_ge(sems["squared"], pe.next("squared"))
                    mm(O[:, i, :], C["ones"], src[:]).then_inc(*pe.tell("l2sum"))
                t_eng.wait_ge(sems["y"], pe.next("y"))
                mm(Et(0), W["out0"][:], ta[:]).then_inc(*pe.tell("yout"))
                layernorm(x[:], "resid")
                t_eng.wait_ge(sems["normed"], pe.next("normed"))
                route(8, W["gate0"][:], RB["L0_ffn_gate_b"])
                turn_weights(8)
                t_eng.wait_ge(sems["wsplit"], pe.next("wsplit"))
                t_eng.wait_ge(sems["y"], pe.next("y"))
                mm(O[:, 0, :], W["expb0"][:], onehot[0:8, :], stop=False)
                m0 = pe.seen.get("masked", 0)
                for e in range(9):
                    if e < 8:
                        if e >= 2:
                            t_eng.wait_ge(sems["masked"], pe.at("masked", m0 + e - 1))
                        mm(Et(e % 2), selb[0:96, e, :], wsp[:, :]).then_inc(*pe.tell("bcast"))
                    if e >= 1:
                        t_eng.wait_ge(sems["masked"], pe.at("masked", m0 + e))
                        mm(O[:, 0, :], W["exp0"][:, e - 1, :], gated[:, (e - 1) % 2, :], start=False, stop=e == 8).then_inc(*pe.tell("out0" if e == 8 else "maskused"))
                layernorm(x[:], "resid")
                t_eng.wait_ge(sems["normed"], pe.next("normed"))
                attention(ATTN["chunk"])
                t_eng.wait_ge(sems["oback"], pe.next("oback", 16))
                mm(Et(0), W["u1"][:], outT).then_inc(*pe.tell("yout"))
                layernorm(x[:], "resid")
                t_eng.wait_ge(sems["normed"], pe.next("normed"))
                attention(ATTN["causal"])
                project(padded["of"], "attn_out")
                rms()
                t_eng.wait_ge(sems["y"], pe.next("y"))
                route(8, W["routef"][:])
                turn_weights(8)
                t_eng.wait_ge(sems["wsplit"], pe.next("wsplit"))
                ffn("dense", acc[:])
                rms()
                t_eng.wait_ge(sems["y"], pe.next("y"))
                ffn("moe1", h[:])
                rms()
                layernorm(x[:], "resid")
                t_eng.wait_ge(sems["normed"], pe.next("normed"))
                for i, n in enumerate(("u2", "q2", "k2")):
                    mm(Et(i), W[n][:], h[:]).then_inc(*pe.tell("l2a"))
                for i, (n, bias) in enumerate((("v2", RB["L2_attn_bv"]), ("k2", RB["L2_attn_bk"]))):
                    for t in range(NT):
                        out = M[:, i, P * t:P * t + P]
                        mm(out, h[:, P * t:P * t + P], W[n][:], stop=False)
                        ins = mm(out, C["ones"][0:1, :], bias, start=False)
                        if t == NT - 1:
                            ins.then_inc(*pe.tell("l2a"))
                t_eng.wait_ge(sems["l2dve"], pe.next("l2dve", 5))
                t_eng.wait_ge(sems["l2act"], pe.next("l2act", 5))
                for j in range(NT - 1):
                    if j:
                        t_eng.wait_ge(sems["statesb"], pe.next("statesb"))
                    mm(O[:, 1, 0:P], ktm[:, j, :], vtm[:, j, :], start=j == 0, stop=True,
                       skip_group_check=True).then_inc(*pe.tell("state"))
                t_eng.wait_ge(sems["statesb"], pe.next("statesb"))

                def energies(n):
                    i, half = divmod(n, 2)
                    for q in range(4):
                        ins = mm(E[:, n % 2, P * q:P * q + P], Kh[:, 4 * half + q, P * i:P * i + P], qe[:, P * i:P * i + P])
                        if q == 3:
                            ins.then_inc(*pe.tell("energy"))

                em0 = pe.seen.get("emask", 0)
                for n in range(2 * NT):
                    if n == 0:
                        energies(0)
                    if n + 1 < 2 * NT:
                        if n >= 1:
                            t_eng.wait_ge(sems["emask"], pe.at("emask", em0 + n))
                        energies(n + 1)
                    i, half = divmod(n, 2)
                    out = O[:, 0, P * i:P * i + P]
                    if half == 0 and i > 0:
                        mm(out, state[:, i - 1, :], qe[:, P * i:P * i + P], stop=False)
                    t_eng.wait_ge(sems["emask"], pe.at("emask", em0 + n + 1))
                    for q in range(4):
                        ins = mm(out, Vz[:, i, 4 * half + q, :], energy[:, n % 2, P * q:P * q + P],
                           start=half == 0 and q == 0 and i == 0, stop=half == 1 and q == 3)
                        if q == 3:
                            ins.then_inc(*pe.tell("l2out" if n == 2 * NT - 1 else "emused"))
                rms()
                t_eng.wait_ge(sems["y"], pe.next("y"))
                mm(Et(0), W["o2"][:], ta[:]).then_inc(*pe.tell("yout"))
                layernorm(x[:], "resid")
                t_eng.wait_ge(sems["normed"], pe.next("normed"))
                route(16, W["gate2"][:])
                turn_weights(16)
                t_eng.wait_ge(sems["wsplit"], pe.next("wsplit"))
                ffn("moe2", h[:])
                layernorm(x[:], "resid")
                t_eng.wait_ge(sems["normed"], pe.next("normed"))
                attention(ATTN["full"])
                project(padded["o3"], "yout")
                layernorm(x[:], "resid")
                t_eng.wait_ge(sems["normed"], pe.next("normed"))
                route(8, W["gate3"][:])
                turn_weights(8)
                t_eng.wait_ge(sems["wsplit"], pe.next("wsplit"))
                ffn("moe3", h[:])
                t_eng.wait_ge(sems["x_stored"], pe.at("x_stored", 16))
            totals["pe"] = pe

        made = {}
        for e in totals.values():
            for n, k in e.made.items():
                made[n] = made.get(n, 0) + k
        return made


_TURNED = ["L0_attn_W_in", "L0_attn_W_out", "L1_attn_wq", "L1_attn_wu", "L2_attn_Wq", "L2_attn_Wk", "L2_attn_Wv",
           "L2_attn_Wu", "L2_attn_Wo", "L2_ffn_gate_w", "L3_attn_Wo", "L3_ffn_gate_w"]
_HEADS = ["L3_attn_Wq", "L3_attn_Wk", "L3_attn_Wv"]
_EXPERTS = ["L3_ffn_w1", "L3_ffn_w2", "L3_ffn_w3"]
_FLAT = ["L3_attn_bq", "L3_attn_bk", "L3_attn_bv"]


def kernel(**inputs):
    import numpy as _np
    import concourse.bacc as _bacc
    from concourse import mybir as _mybir
    from concourse.bass_utils import run_bass_kernel_spmd as _run

    nc = _bacc.Bacc("TRN2", target_bir_lowering=False, num_devices=1)
    arrays, args = {}, {}

    def declare(name, a):
        a = _np.ascontiguousarray(a)
        arrays["in_" + name] = a
        return nc.dram_tensor("in_" + name, a.shape, _mybir.dt.from_np(a.dtype), kind="ExternalInput").ap()

    for name, a in inputs.items():
        a = _np.asarray(a)
        if name == "L0_attn_X":
            x_in = declare(name, a.transpose(0, 2, 1))
            continue
        if name in _TURNED:
            a = a.T
        elif name in _HEADS:
            a = a.reshape(P, P).T
        elif name in _EXPERTS:
            a = a.transpose(2, 0, 1)
        elif name in _FLAT:
            a = a.reshape(P)
        args[name] = declare(name, a)
    const = declare("constants", constant_table())
    x_out = nc.dram_tensor("out_0", (NB, P, S), _mybir.dt.float32, kind="ExternalOutput").ap()
    made = network(nc, args, const, x_in, x_out)
    assert made == EVENTS, made
    r = _run(nc, [arrays], core_ids=[0])
    return _np.ascontiguousarray(r.results[0]["out_0"].transpose(0, 2, 1))
```

```python
from contextlib import ExitStack

import concourse.bass as bass
from concourse import mybir
import numpy as np

F32 = mybir.dt.float32
BF16 = mybir.dt.bfloat16
I32 = mybir.dt.int32
ALU = mybir.AluOpType
ACT = mybir.ActivationFunctionType
AX_X = mybir.AxisListType.X

P = 128
NB = 8
STREAMS = 2
TURNS = NB // STREAMS
S = 512
NT = S // P
UNITS = 16
HD = 8
GROUPS = UNITS // 4
ROT = P // 2
STACK = 6 * HD
ROWS = STACK + 2
NEG = -1.0e30
PRODUCTS = ((0, 0), (0, 1), (1, 0), (0, 2), (2, 0), (1, 1))

CONSTS = {}
_at = 0
for _name, _width in (("mean", P), ("ones", P), ("ident", P), ("rot", P), ("cos", S), ("sin", S), ("block", P),
                      ("head", 8), ("den", GROUPS), ("tril", P), ("tri8", 64), ("tri16", 256), ("own", 2), ("carry", 2),
                      ("upper", P), ("lower", P), ("sel", 8 * P), ("pair", 8 * P), ("stack", 8 * 2 * 3 * P)):
    CONSTS[_name] = (_at, _width)
    _at += _width
CONST_WIDTH = _at
RESIDENT = CONSTS["upper"][0]


def constant_table():
    c = {n: np.zeros((P, w), np.float32) for n, (_, w) in CONSTS.items()}
    i = np.arange(P)
    c["mean"][:] = 1.0 / P
    c["ones"][:] = 1.0
    c["ident"][i, i] = 1.0
    for a in range(0, ROT, 2):
        c["rot"][a + 1, a] = -1.0
        c["rot"][a, a + 1] = 1.0
    inv = (1.0 / np.float32(10000.0) ** (np.arange(0, ROT, 2, dtype=np.float32) / np.float32(ROT))).astype(np.float32)
    freqs = np.repeat(np.arange(S, dtype=np.float32)[:, None] * inv[None, :], 2, axis=-1)
    c["cos"][:] = 1.0
    c["cos"][:ROT] = np.cos(freqs).T
    c["sin"][:ROT] = np.sin(freqs).T
    c["block"][:] = (i[:, None] // 16) == (i[None, :] // 16)
    c["head"][:] = (i[:, None] // 16) == np.arange(8)[None, :]
    c["den"][:] = i[:, None] == np.arange(GROUPS)[None, :] * 32 + HD
    c["tril"][:] = i[:, None] <= i[None, :]
    for n, e in (("tri8", 8), ("tri16", 16)):
        c[n][:] = (np.arange(e)[None, :] < np.arange(e)[:, None]).reshape(1, e * e)
    c["upper"][:] = np.where(i[None, :] > i[:, None], NEG, 0.0)
    c["lower"][:] = np.where(i[None, :] < i[:, None], NEG, 0.0)
    c["own"][:] = i[:, None] // 64 == np.arange(2)
    c["carry"][:] = c["own"] * ((i % 64 >= STACK) & (i % 64 < ROWS))[:, None]
    stack = c["stack"].reshape(P, 8, 2, 3, 2, 64)
    for slot, parts in enumerate(PRODUCTS):
        for side, part in enumerate(parts):
            for u in range(UNITS):
                for d in range(HD):
                    stack[HD * u + d, u // 2, side, part, u % 2, HD * slot + d] = 1.0
    sel = c["sel"].reshape(P, 8, P)
    pair = c["pair"].reshape(P, 8, P)
    for part in range(3):
        for e in range(8):
            sel[32 * part + e, e, :] = 1.0
            pair[32 * part + 2 * e, e, :64] = 1.0
            pair[32 * part + 2 * e + 1, e, 64:] = 1.0
    return np.concatenate([c[n] for n in CONSTS], axis=1)


EVENTS = dict(
    x_loaded=16, mstaged=96, mstacked=96, ostaged=256, oback=16, x_stored=16, window=192, l2z=1, squared=15,
    copied=7, part1=5, stacked=72, prob=192, widened=12, expd=3, tanh=37, l2act=5, centred=9, dve_step=234,
    rstd=14, normed=9, rotated=2, y=5, resid=8, wtm=4, wsplit=4, masked=16, vready=18, bank_read=140,
    msplit=3, rden=3, onorm=12, expin=2, gate_used=37, gated=37, weighted=24, l2dve=15, statesb=3, mean=9,
    var=14, rbroad=14, qkv=3, turned=2, yout=4, logits=4, wT=4, bcast=32, maskused=14, out0=1, proj=5, vtm=3,
    raised=48, sc1=128, mT=3, sc2=192, pv=48, den=3, dbroad=12, attn_out=1, gate=37, up=37, used=33,
    dense_out=1, moe1_out=1, l2a=5, state=3, energy=8, l2out=1, moe2_out=1, moe3_out=1,
)


class Count:

    def __init__(self, sems, chain, when=None, stream=0):
        self.sems, self.chain, self.when, self.stream = sems, chain, when, stream
        self.seen, self.made, self.last = {}, {}, None

    def value(self, name, count):
        turn = self.when.turn if self.when else 0
        if isinstance(turn, int):
            return turn * EVENTS[name] + count if turn else count
        return (turn + self.stream) * EVENTS[name] + (count - self.stream * EVENTS[name])

    def at(self, name, count):
        self.seen[name] = max(self.seen.get(name, 0), count)
        return self.value(name, count)

    def next(self, name, n=1):
        return self.at(name, self.seen.get(name, 0) + n)

    def tell(self, name=None, n=1):
        name = name or self.chain
        self.made[name] = self.made.get(name, 0) + n
        self.last = (name, self.made[name])
        return self.sems[name], n

    def own(self):
        name, count = self.last
        return self.sems[name], self.value(name, count)



class When:

    def __init__(self, turn):
        self.turn = turn


def advance(program, steps=None):
    done = object()
    written = 0
    while written != steps and next(program, done) is not done:
        written += 1
    return written


def begin_turns(stream):
    when = When(0)
    first = stream(0, when)
    advance(first, LAG)
    return first, when


def run_turn(stream, first, when, turn):
    when.turn = turn
    second = stream(1, When(turn))
    while advance(first, 1):
        advance(second, 1)
    when = When(turn + 1)
    first = stream(0, when)
    for _ in range(LAG):
        advance(first, 1)
        advance(second, 1)
    assert not advance(second)
    return first, when


def idle(n):
    for _ in range(n):
        yield


LAG = 20
NORM, ROUTE = 4, 4
STACKING = UNITS // 2
MAXIMA = 4
PASS = UNITS
SPLITTING = 2
BEFORE_MAXIMA = SPLITTING + STACKING + PASS
OUTPUTS = 6
SPREAD = 1
STEPS_0 = (2 * NORM + 5) + (NORM + ROUTE + 9)
STEPS_1F = NORM + ROUTE + (2 * 4 + 1) + NORM + (2 * 8 + 1) + NORM
STEPS_2 = 2 * NORM + 5 + (NT - 1 + 2 * NT) * SPREAD
STEPS_2F = NORM + ROUTE + (2 * 9 + 1)
STEPS_3F = 1 + NORM + ROUTE + (2 * 16 + 1)
assert NORM + STEPS_2 + NORM + ROUTE >= LAG


class Stream:
    pass


def network(nc, inp, const, x_in, x_out):
    ctx = ExitStack()
    with ctx:
        def sb(name, shape, dt=F32):
            return ctx.enter_context(nc.sbuf_tensor(name, shape, dt))

        W = {}
        first_loads, loads = [], []

        def weight(name, shape, src):
            W[name] = sb("w_" + name, shape)
            (first_loads if name in ("in0", "out0", "gate0") else loads).append((W[name][:], src))

        cs = sb("cs", [P, RESIDENT])
        first_loads.append((cs[:], const[:, 0:RESIDENT]))
        C = {n: cs[:, a:a + w] for n, (a, w) in CONSTS.items() if a < RESIDENT}

        weight("in0", [P, 3 * P], inp["L0_attn_W_in"])
        weight("out0", [P, P], inp["L0_attn_W_out"])
        weight("gate0", [P, 8], inp["L0_ffn_gate_w"])
        weight("exp0", [P, 8, P], inp["L0_ffn_expert_w"].rearrange("e d h -> d e h"))
        weight("expb0", [8, P], inp["L0_ffn_expert_b"])
        weight("q1", [P, P], inp["L1_attn_wq"])
        weight("u1", [P, P], inp["L1_attn_wu"])
        for n in "qkv":
            weight(n + "f", [P, P], inp["L1_ffn_w" + n])
        weight("routef", [P, 8], inp["L1_ffn_router_w"])
        for n in "qkvuo":
            weight(n + "2", [P, P], inp["L2_attn_W" + n])
        weight("gate2", [P, 16], inp["L2_ffn_gate_w"])
        weight("ws2", [P, P], inp["L2_ffn_ws_in"])
        weight("vs2", [P, P], inp["L2_ffn_vs_in"])
        weight("wso2", [P, P], inp["L2_ffn_ws_out"])
        for n in "qkv":
            weight(n + "3", [P, P], inp["L3_attn_W" + n])
        weight("gate3", [P, 8], inp["L3_ffn_gate_w"])

        padded = {}
        for n, key in (("of", "L1_ffn_wo"), ("o3", "L3_attn_Wo")):
            padded[n] = sb("w_" + n, [P, GROUPS, P])
            src = inp[key].rearrange("(g c d) n -> c d g n", g=GROUPS, c=4)
            for c in range(4):
                loads.append((padded[n][32 * c:32 * c + HD, :, :], src[c]))

        window = sb("window", [P, 3 * 2048])
        WINDOWS = []
        for group in ([("w1f", [4 * P], inp["L1_ffn_w1"]),
                       ("w3f", [4 * P], inp["L1_ffn_w3"]),
                       ("w2f", [4, P], inp["L1_ffn_w2"].rearrange("(b p) d -> p b d", p=P)),
                       ("ew1f", [8, P], inp["L1_ffn_ew1"].rearrange("e d h -> d e h")),
                       ("ew3f", [8, P], inp["L1_ffn_ew3"].rearrange("e d h -> d e h")),
                       ("ew2f", [8, P], inp["L1_ffn_ew2"].rearrange("e h d -> h e d"))],
                      [("ewin2", [16, 64], inp["L2_ffn_e_win"].rearrange("e d h -> d e h")),
                       ("evin2", [16, 64], inp["L2_ffn_e_vin"].rearrange("e d h -> d e h")),
                       ("ewout2", [8, P], inp["L2_ffn_e_wout"].rearrange("(p two) h d -> (two h) p d", two=2))],
                      [("w13", [8, 256], inp["L3_ffn_w1"]),
                       ("w33", [8, 256], inp["L3_ffn_w3"]),
                       ("w23", [2, 8, P], inp["L3_ffn_w2"].rearrange("(b p) e d -> p b e d", p=P))]):
            at, loads_of = 0, []
            for n, shape, src in group:
                width = int(np.prod(shape))
                flat = window[:, at:at + width]
                W[n] = flat if len(shape) == 1 else flat.rearrange("p (a b) -> p a b", a=shape[0]) \
                    if len(shape) == 2 else flat.rearrange("p (a b c) -> p a b c", a=shape[0], b=shape[1])
                at += width
                loads_of.append((W[n], src))
            WINDOWS.append(loads_of)
        IN_WINDOW = [16 * sum(len(g) for g in WINDOWS[:i + 1]) for i in range(3)]

        VEC = ["L0_attn_ln_g", "L0_attn_ln_b", "L1_attn_bq", "L1_attn_bu", "L1_ffn_attn_norm_w", "L1_ffn_ff_norm_w",
               "L1_ffn_moe_norm_w", "L2_attn_bq", "L2_attn_bk", "L2_attn_bu", "L2_attn_bo", "L2_attn_scale",
               "L3_attn_bq", "L3_attn_bk", "L3_attn_bo"]
        vecs = sb("vecs", [P, len(VEC) + 1])
        V = {}
        for i, n in enumerate(VEC):
            V[n] = vecs[:, i:i + 1]
            (first_loads if n.startswith("L0") else loads).append((V[n], inp[n].rearrange("(p one) -> p one", one=1)))
        half_bu = vecs[:, len(VEC):len(VEC) + 1]
        ROWB = ["L1_attn_bq", "L2_attn_bk", "L2_attn_bv", "L3_attn_bv", "L0_ffn_gate_b"]
        rows = sb("rows", [1, len(ROWB), P])
        RB = {}
        for i, n in enumerate(ROWB):
            w = inp[n].shape[0]
            RB[n] = rows[0:1, i, 0:w]
            (first_loads if n.startswith("L0") else loads).append((RB[n], inp[n].rearrange("(one n) -> one n", one=1)))

        identb = sb("identb", [P, P], BF16)
        upperb = sb("upperb", [P, P], BF16)
        lowerb = sb("lowerb", [P, P], BF16)
        selb = sb("selb", [P, 8, P], BF16)
        pairb = sb("pairb", [P, 8, P], BF16)
        stackb = sb("stackb", [P, 8, 2, 3, P], BF16)

        NAMES = ["x_loaded", "x_stored", "act_step", "dve_step", "pool_step",
                 "mean", "centred", "squared", "var", "rstd", "rbroad", "normed", "resid",
                 "qkv", "copied", "turned", "rotated", "y", "yout",
                 "logits", "expin", "expd", "wtm", "wT", "wsplit",
                 "gate", "tanh", "gate_used", "bcast", "weighted", "up", "gated", "used",
                 "dense_out", "moe1_out", "moe2_out", "moe3_out", "attn_out", "out0", "masked", "maskused",
                 "proj", "part1", "raised", "stacked", "vtm", "vready",
                 "sc1", "bank_read", "mT", "msplit", "mstaged", "mstacked", "sc2", "prob", "pv",
                 "den", "rden", "widened", "dbroad", "onorm", "ostaged", "oback",
                 "l2a", "l2act", "l2dve", "l2z", "state", "statesb", "energy", "l2out"]
        shared = {n: ctx.enter_context(nc.semaphore("s_" + n)) for n in ("first_loaded", "w_loaded", "zeroed", "consts", "paced",
                                                                         "window")}
        Z = []
        for i in range(STREAMS):
            z = Stream()
            Z.append(z)

            def own(name, shape, dt=F32, i=i):
                return sb(f"{name}_{i}", shape, dt)

            z.x = own("x", [P, S])
            z.h = own("h", [P, S])
            z.xc, z.sq = own("xc", [P, S]), own("sq", [P, S])
            z.osum = own("osum", [P, GROUPS, S])
            z.tanh, z.gated = z.osum[:, 0:2, :], z.osum[:, 2:4, :]
            z.stat = own("stat", [P, 8, NT])
            z.stacks = own("stacks", [P, 3, UNITS // 2, S], BF16)
            z.Q, z.K = z.stacks[:, 0], (z.stacks[:, 1], z.stacks[:, 2])
            spare = z.stacks[:, 2].rearrange("p a b -> p (a b)").bitcast(F32).rearrange("p (a b) -> p a b", b=S)
            z.acc = spare[:, 0]
            z.rs, z.ta, z.tb = spare[:, 1], spare[:, 2], spare[:, 3]
            z.Vp = own("Vp", [P, NT, UNITS, 32])
            z.probs = own("probs", [P, 8, S])
            z.parts = z.probs[:, 0:3, :].rearrange("p a s -> p (a s)").bitcast(BF16) \
                .rearrange("p (i a s) -> p i a s", i=2, a=3)
            z.residue = z.probs[:, 4:6, :]
            z.mx = own("mx", [P, NT, UNITS])
            z.msp = z.sq[0:64, :].bitcast(BF16).rearrange("p (a b) -> p a b", a=2)
            z.rinv16 = own("rinv16", [P, GROUPS, NT, 4])
            z.lg, z.pr = own("lg", [P, NT, 16]), own("pr", [P, NT, 16])
            z.cmp = z.tanh.rearrange("p a b -> p (a b)")
            z.eqs = z.gated.rearrange("p a b -> p (a b)")
            z.rank = own("rank", [P, NT, 16])
            z.red, z.rinv = own("red", [P, NT]), own("rinv", [P, NT])
            z.wtm = own("wtm", [P, NT, 16])
            z.wsp = own("wsp", [96, S], BF16)
            z.wres = z.xc[0:16, :]
            z.wmid = z.sq[0:16, 0:S // 2].bitcast(BF16)
            z.onehot = z.tb[0:16, :]
            z.unit1 = own("unit1", [P, 1])
            z.vsb = z.probs[:, 6, :]
            z.Kh = z.stacks[:, 0:2].rearrange("p i a b -> p (i a b)").bitcast(F32) \
                .rearrange("p (h s) -> p h s", h=8)
            z.Vz = z.probs[:, :, :].rearrange("p a b -> p (a b)").rearrange("p (t h d) -> p t h d", t=NT, h=8)
            z.qe, z.ke = z.sq, z.rs
            z.ktm = z.xc[:, :].rearrange("p (t d) -> p t d", t=NT)
            z.state = z.tb[:, :].rearrange("p (t d) -> p t d", t=NT)
            z.uu = z.acc
            z.vtm = z.osum[:, 2, :]
            z.energy = z.osum[:, 0:2, :]
            z.utanh = z.osum[:, 3, :]
            z.vtanh = z.ta
            z.outT = z.tb
            z.hw = z.sq
            z.bank = ctx.enter_context(nc.psum_tensor(f"bank_{i}", [P, 4, S], F32))
            z.minus_dram = nc.dram_tensor(f"minus_dram_{i}", (2, UNITS, S), BF16).ap()
            z.out_dram = nc.dram_tensor(f"out_dram_{i}", (P, S), F32).ap()
            z.sems = {n: ctx.enter_context(nc.semaphore(f"s_{n}_{i}")) for n in NAMES} | shared
        passing = Z[1].probs[:, :, :].rearrange("p a c -> p (a c)")[:, 0:CONSTS["stack"][0] - RESIDENT]
        split = CONSTS["stack"][0]
        loads.append((passing, const[:, RESIDENT:split]))
        C.update({n: passing[:, a - RESIDENT:a - RESIDENT + w] for n, (a, w) in CONSTS.items() if RESIDENT <= a < split})
        C["stack"] = Z[1].stacks[:, :, :, :].rearrange("p i a b -> p (i a b)").bitcast(F32)
        loads.append((C["stack"], const[:, split:]))
        n_loads = len(loads)
        ZEROED, FILLS = 2 + STREAMS, 2 * STREAMS
        CONSTS_READY = FILLS + 7
        counts = {}

        ATTN = {
            "chunk": dict(causal=False, chunk=True, scale=float(P) ** -0.5, q="q1", bq=V["L1_attn_bq"], k=None, bk=None,
                          v="q1", bv=RB["L1_attn_bq"]),
            "causal": dict(causal=True, chunk=False, scale=float(HD) ** -0.5, q="qf", bq=None, k="kf", bk=None,
                           v="vf", bv=None),
            "full": dict(causal=False, chunk=False, scale=float(HD) ** -0.5, q="q3", bq=V["L3_attn_bq"], k="k3",
                         bk=V["L3_attn_bk"], v="v3", bv=RB["L3_attn_bv"]),
        }

        def ffn_blocks(kind):
            if kind == "dense":
                return [(W["w1f"][:, P * b:P * b + P], W["w3f"][:, P * b:P * b + P], None, W["w2f"][:, b, :])
                        for b in range(4)]
            if kind == "moe1":
                return [(W["ew1f"][:, e, :], W["ew3f"][:, e, :], selb[0:96, e, :], W["ew2f"][:, e, :])
                        for e in range(8)]
            if kind == "moe2":
                pairs = [(W["ewin2"][:, 2 * e:2 * e + 2, :].rearrange("p a b -> p (a b)"),
                          W["evin2"][:, 2 * e:2 * e + 2, :].rearrange("p a b -> p (a b)"),
                          pairb[0:96, e, :], W["ewout2"][:, e, :]) for e in range(8)]
                return [(W["ws2"][:], W["vs2"][:], None, W["wso2"][:])] + pairs
            return [(W["w13"][:, e, P * b:P * b + P], W["w33"][:, e, P * b:P * b + P], None if b else selb[0:96, e, :],
                     W["w23"][:, b, e, :]) for e in range(8) for b in range(2)]

        def qcols(kt, causal):
            return slice(P * kt if causal else 0, S)

        def q_stack(z, u):
            return z.Q[:, u // 2, :]

        def k_stack(z, u):
            return z.K[u % 2][:, u // 2, :]

        block = ctx.enter_context(nc.Block())


        @block.sync
        def _(sp_eng):
            for dst, src in first_loads:
                sp_eng.dma_start(dst, src).then_inc(shared["first_loaded"], 16)

            def stream(i, when):
                z = Z[i]
                sems = z.sems
                sp = Count(sems, None, when, i)
                counts.setdefault(("sp", i), sp)
                dma = sp_eng.dma_start

                def lower_maxima(cfg):
                    sp_eng.wait_ge(sems["msplit"], sp.next("msplit"))
                    for part in range(2):
                        if cfg["chunk"]:
                            dma(z.minus_dram[part].rearrange("c (q m) -> q c m", q=NT), z.msp[0:NT * UNITS, part, 0:P]).then_inc(*sp.tell("mstaged", 16))
                        else:
                            dma(z.minus_dram[part], z.msp[0:UNITS, part, :]).then_inc(*sp.tell("mstaged", 16))
                    yield
                    sp_eng.wait_ge(sems["mstaged"], sp.next("mstaged", 32))
                    for odd in range(2):
                        dma(z.Q[64 * odd + STACK:64 * odd + ROWS, :, :], z.minus_dram[:, odd:UNITS:2, :]).then_inc(*sp.tell("mstacked", 16))
                    yield from idle(MAXIMA - 1 + PASS + 3)

                dma(z.x[:], x_in[TURNS * i + when.turn]).then_inc(*sp.tell("x_loaded", 16))
                yield from idle(STEPS_0 + NORM + BEFORE_MAXIMA)
                yield from lower_maxima(ATTN["chunk"])
                sp_eng.wait_ge(sems["onorm"], sp.next("onorm", GROUPS))
                for c in range(4):
                    for g in range(GROUPS):
                        tok = P * g + 32 * c
                        dma(z.out_dram[:, tok:tok + 32].rearrange("(j d) t -> d j t", d=HD),
                            z.osum[32 * c:32 * c + HD, g, :].rearrange("d (j t) -> d j t", t=32)).then_inc(*sp.tell("ostaged", 16))
                yield
                sp_eng.wait_ge(sems["ostaged"], sp.next("ostaged", 16 * 16))
                dma(z.outT[:], z.out_dram).then_inc(*sp.tell("oback", 16))
                yield from idle(OUTPUTS)
                yield from idle(1 + NORM + BEFORE_MAXIMA)
                yield from lower_maxima(ATTN["causal"])
                yield from idle(STEPS_1F + STEPS_2 + STEPS_2F + NORM + BEFORE_MAXIMA)
                yield from lower_maxima(ATTN["full"])
                yield from idle(STEPS_3F)
                sp_eng.wait_ge(sems["resid"], sp.next("resid", 8))
                dma(x_out[TURNS * i + when.turn], z.x[:]).then_inc(*sp.tell("x_stored", 16))
                yield
                sp_eng.wait_ge(sems["x_stored"], sp.at("x_stored", 16))
                sp_eng.sem_inc(shared["paced"], 1)

            ahead, when = begin_turns(stream)
            sp_eng.wait_ge(shared["zeroed"], ZEROED)
            for dst, src in loads:
                sp_eng.dma_start(dst, src).then_inc(shared["w_loaded"], 16)
            sp_eng.wait_ge(shared["consts"], CONSTS_READY)
            with sp_eng.Fori(0, TURNS) as turn:
                ahead, when = run_turn(stream, ahead, when, turn)

        @block.gpsimd
        def _(pool_eng):
            pool0 = Count(shared, None)

            def fill(dst, value, name):
                pool_eng.memset(dst, value).then_inc(*pool0.tell(name))
                pool_eng.wait_ge(*pool0.own())

            for t in (padded["of"], padded["o3"], Z[0].wsp, Z[1].wsp):
                fill(t[:], 0.0, "zeroed")
            for z in Z:
                fill(z.Vp[:, :, :, HD:HD + 1], 1.0, "consts")
                fill(z.Vp[:, :, :, HD + 1:32], 0.0, "consts")

            with pool_eng.Fori(0, TURNS) as turn:
                pool = [Count(z.sems, "pool_step", When(turn), i) for i, z in enumerate(Z)]
                weights = counts["pool", "window"] = Count(shared, None, When(turn))
                for i in range(STREAMS):
                    counts["pool", i] = pool[i]

                def load_window(k):
                    for dst, src in WINDOWS[k]:
                        pool_eng.dma_start(dst, src).then_inc(*weights.tell("window", 16))

                load_window(0)
                for z, count in zip(Z, pool):
                    pool_eng.wait_ge(z.sems["onorm"], count.next("onorm", 2 * GROUPS))
                    pool_eng.sem_inc(shared["paced"], 1)
                    pool_eng.memset(z.probs[:], 0.0).then_inc(*count.tell("l2z"))
                    pool_eng.wait_ge(*count.own())
                    pool_eng.sem_inc(shared["paced"], 1)
                for z, count in zip(Z, pool):
                    pool_eng.wait_ge(z.sems["moe1_out"], count.next("moe1_out"))
                    pool_eng.sem_inc(shared["paced"], 1)
                load_window(1)
                for z, count in zip(Z, pool):
                    pool_eng.wait_ge(z.sems["moe2_out"], count.next("moe2_out"))
                    pool_eng.sem_inc(shared["paced"], 1)
                load_window(2)
                for z, count in zip(Z, pool):
                    pool_eng.wait_ge(z.sems["x_stored"], count.at("x_stored", 16))
                    pool_eng.sem_inc(shared["paced"], 1)

        @block.scalar
        def _(act_eng):
            act_eng.wait_ge(shared["first_loaded"], 16 * len(first_loads))
            run = act_eng.activation

            def stream(i, when):
                z = Z[i]
                sems = z.sems
                act = Count(sems, "act_step", when, i)
                counts.setdefault(("act", i), act)
                B = [z.bank[:, k, :] for k in range(4)]

                def layernorm():
                    act_eng.wait_ge(sems["centred"], act.next("centred"))
                    run(z.sq[:], z.xc[:], ACT.Square).then_inc(*act.tell("squared"))
                    yield from idle(NORM)

                def rms(bank, name):
                    act_eng.wait_ge(sems[name], act.next(name))
                    run(z.sq[:], bank, ACT.Square).then_inc(*act.tell("squared"))
                    run(z.ta[:], bank, ACT.Copy).then_inc(*act.tell("copied"))
                    yield from idle(NORM)

                def softmax_exp(n):
                    act_eng.wait_ge(sems["expin"], act.next("expin"))
                    run(z.pr[:, :, 0:n], z.lg[:, :, 0:n], ACT.Exp).then_inc(*act.tell("expd"))
                    yield from idle(ROUTE)

                def ffn(kind):
                    gated0 = act.seen.get("gated", 0)
                    for i in range(len(ffn_blocks(kind))):
                        act_eng.wait_ge(sems["gate"], act.next("gate"))
                        if i >= 2:
                            act_eng.wait_ge(sems["gated"], act.at("gated", gated0 + i - 1))
                        run(z.tanh[:, i % 2, :], B[0], ACT.Tanh, scale=0.5).then_inc(*act.tell("tanh"))
                        yield from idle(2)
                    act.seen["gated"] = gated0 + len(ffn_blocks(kind))
                    yield

                def attention(cfg):
                    sides = 1 if cfg["chunk"] else 2
                    for side in range(sides):
                        act_eng.wait_ge(sems["proj"], act.next("proj"))
                        bias = cfg["bq"] if side == 0 else cfg["bk"]
                        run(z.parts[:, side, 0, :], B[side], ACT.Identity,
                            **({} if bias is None else {"bias": bias})).then_inc(*act.tell("part1"))
                    yield from idle(SPLITTING)
                    for n in range(UNITS):
                        pair, side = divmod(n, 2)
                        if cfg["chunk"]:
                            def unit_pair(stack):
                                return stack.rearrange("p c (j t) -> p j c t", t=32)[:, 2 * pair:2 * pair + 2]
                            src = B[n % 4].rearrange("p (j c t) -> p j c t", j=2, t=32)
                        else:
                            def unit_pair(stack):
                                return stack[:, pair, :]
                            src = B[n % 4]
                        act_eng.wait_ge(sems["raised"], act.next("raised"))
                        if side == 0:
                            run(unit_pair(z.Q), src, ACT.Copy).then_inc(*act.tell("stacked"))
                        else:
                            for odd in range(2):
                                run(unit_pair(z.K[odd]), src, ACT.Identity, scale=C["own"][:, odd:odd + 1],
                                    bias=C["carry"][:, odd:odd + 1]).then_inc(*act.tell("stacked"))
                            yield
                    yield from idle(PASS + MAXIMA)
                    n0 = act.seen.get("pv", 0)
                    for n in range(GROUPS * NT):
                        q = qcols(n % NT, cfg["causal"])
                        if n >= 2:
                            act_eng.wait_ge(sems["pv"], act.at("pv", n0 + n - 1))
                        for c in range(4):
                            act_eng.wait_ge(sems["sc2"], act.next("sc2"))
                            run(z.probs[:, 4 * (n % 2) + c, q], B[(4 * n + c) % 3][:, q], ACT.Exp, scale=cfg["scale"]).then_inc(*act.tell("prob"))
                        yield
                    act.seen["pv"] = n0 + GROUPS * NT
                    yield from idle(2)
                    act_eng.wait_ge(sems["rden"], act.next("rden"))
                    for g in range(GROUPS):
                        run(z.probs[:, g, :].rearrange("p (t c w) -> p t c w", t=NT, c=4),
                            z.rinv16[:, g].unsqueeze(3).broadcast_to([P, NT, 4, 32]), ACT.Copy).then_inc(*act.tell("widened"))
                    yield

                yield from layernorm()
                yield from layernorm()
                for k, dst in enumerate((z.ta[:], z.tb[:], z.vsb)):
                    act_eng.wait_ge(sems["qkv"], act.next("qkv"))
                    run(dst, B[k], ACT.Copy).then_inc(*act.tell("copied"))
                yield
                for k, dst in enumerate((z.sq, z.xc)):
                    act_eng.wait_ge(sems["rotated"], act.next("rotated"))
                    run(dst[:], z.residue[:, k, :], ACT.Square).then_inc(*act.tell("squared"))
                yield from idle(4)
                yield from layernorm()
                yield from idle(ROUTE + 9)
                yield from layernorm()
                yield from attention(ATTN["chunk"])
                yield from idle(OUTPUTS + 2)
                yield from layernorm()
                yield from attention(ATTN["causal"])
                yield from rms(B[0], "attn_out")
                yield from softmax_exp(8)
                for kind in ("dense", "moe1"):
                    yield from ffn(kind)
                    yield from rms(B[3], kind + "_out")
                yield from layernorm()
                for src, dst, bias in ((B[0], z.qe[:], V["L2_attn_bq"]), (B[1], z.ke[:], V["L2_attn_bk"]),
                                       (B[2], z.xc[:], None)):
                    act_eng.wait_ge(sems["l2a"], act.next("l2a"))
                    if bias is None:
                        run(dst, src, ACT.Exp).then_inc(*act.tell("l2act"))
                    else:
                        run(dst, src, ACT.Exp, bias=bias).then_inc(*act.tell("l2act"))
                act_eng.wait_ge(sems["l2a"], act.next("l2a"))
                run(z.vtanh[:], B[3], ACT.Tanh, scale=0.5).then_inc(*act.tell("l2act"))
                yield from idle(2)
                act_eng.wait_ge(sems["l2a"], act.next("l2a"))
                run(z.utanh, B[0], ACT.Tanh, scale=0.5, bias=half_bu).then_inc(*act.tell("l2act"))
                yield from idle(STEPS_2 - NORM - 2 - NORM - 1)
                yield from rms(B[3], "l2out")
                yield
                yield from layernorm()
                act_eng.wait_ge(sems["logits"], act.at("logits", 3))
                run(z.pr[:, :, 0:16], z.bank[:, 0, 0:64].rearrange("p (t e) -> p t e", t=NT), ACT.Tanh, scale=0.5).then_inc(*act.tell("expd"))
                yield from idle(ROUTE)
                yield from ffn("moe2")
                yield from layernorm()
                yield from attention(ATTN["full"])
                yield
                yield from layernorm()
                yield from softmax_exp(8)
                yield from ffn("moe3")
                yield

            ahead, when = begin_turns(stream)
            act_eng.wait_ge(shared["w_loaded"], 16 * n_loads)
            act_eng.wait_ge(shared["consts"], CONSTS_READY)
            with act_eng.Fori(0, TURNS) as turn:
                ahead, when = run_turn(stream, ahead, when, turn)

        @block.vector
        def _(v):
            v.wait_ge(shared["first_loaded"], 16 * len(first_loads))
            tt, stt = v.tensor_tensor, v.scalar_tensor_tensor

            def ts(out, a, s1, s2, op0, op1):
                return v.tensor_scalar(out, a, s1, None, op0) if op1 is None else \
                    v.tensor_scalar(out, a, s1, s2, op0, op1)

            def stream(i, when):
                z = Z[i]
                sems = z.sems
                dve = Count(sems, "dve_step", when, i)
                counts.setdefault(("dve", i), dve)
                B = [z.bank[:, k, :] for k in range(4)]
                x, h, acc, xc, ta, tb = z.x, z.h, z.acc, z.xc, z.ta, z.tb

                stat = z.stat[:, :, :].rearrange("p a b -> p (a b)")

                def rsqrt(n, eps, name="rstd"):
                    var, y, t = stat[:, 0:n], stat[:, 8:8 + n], stat[:, 16:16 + n]
                    ts(var, B[1][:, 0:n], eps, None, ALU.add, None).then_inc(*dve.tell())
                    v.wait_ge(*dve.own())
                    ts(y.bitcast(I32), var.bitcast(I32), -0.5, float(0x5f3759df), ALU.mult, ALU.add).then_inc(*dve.tell())
                    for step in range(3):
                        v.wait_ge(*dve.own())
                        tt(t, y, y, ALU.mult).then_inc(*dve.tell())
                        v.wait_ge(*dve.own())
                        stt(t, t, -0.5, var, ALU.mult, ALU.mult).then_inc(*dve.tell())
                        v.wait_ge(*dve.own())
                        stt(y, t, 1.5, y, ALU.add, ALU.mult).then_inc(*dve.tell(name if step == 2 else None))

                def layernorm(src, dst, first=False, gain=None, bias=None):
                    if first:
                        v.wait_ge(sems["x_loaded"], dve.at("x_loaded", 16))
                    v.wait_ge(sems["mean"], dve.next("mean"))
                    tt(xc[:], src, B[0], ALU.subtract).then_inc(*dve.tell("centred"))
                    yield from idle(2)
                    v.wait_ge(sems["var"], dve.next("var"))
                    rsqrt(4, 1e-5)
                    yield
                    v.wait_ge(sems["rbroad"], dve.next("rbroad"))
                    if gain is None:
                        tt(dst, xc[:], B[0], ALU.mult).then_inc(*dve.tell("normed"))
                    else:
                        tt(dst, xc[:], B[0], ALU.mult).then_inc(*dve.tell())
                        v.wait_ge(*dve.own())
                        ts(dst, dst, gain, bias, ALU.mult, ALU.add).then_inc(*dve.tell("normed"))
                    yield

                def top(n, k, src, name=None):
                    p = src[:, :, 0:n]
                    others = p.unsqueeze(2).broadcast_to([P, NT, n, n])
                    mine = p.unsqueeze(3).broadcast_to([P, NT, n, n])
                    tri = C[f"tri{n}"].rearrange("p (a b) -> p a b", a=n).unsqueeze(1).broadcast_to([P, NT, n, n])
                    cv = z.cmp[:, 0:NT * n * n] \
                        .rearrange("p (t a b) -> p t a b", t=NT, a=n)
                    ev = z.eqs[:, 0:NT * n * n] \
                        .rearrange("p (t a b) -> p t a b", t=NT, a=n)
                    yield
                    tt(ev, others, mine, ALU.is_equal).then_inc(*dve.tell())
                    tt(cv, others, mine, ALU.is_gt).then_inc(*dve.tell())
                    v.wait_ge(*dve.own())
                    tt(ev, ev, tri, ALU.mult).then_inc(*dve.tell())
                    v.wait_ge(*dve.own())
                    tt(cv, cv, ev, ALU.add).then_inc(*dve.tell())
                    yield
                    v.wait_ge(*dve.own())
                    v.tensor_reduce(z.rank[:, :, 0:n], cv, AX_X, ALU.add).then_inc(*dve.tell())
                    v.wait_ge(*dve.own())
                    stt(z.wtm[:, :, 0:n], z.rank[:, :, 0:n], float(k), p, ALU.is_lt, ALU.mult).then_inc(*dve.tell(name))
                    v.wait_ge(*dve.own())

                def softmax(n):
                    lp = z.bank[:, 0, 0:NT * n].rearrange("p (t e) -> p t e", t=NT)
                    v.wait_ge(sems["logits"], dve.next("logits"))
                    v.tensor_reduce(z.red[:], lp, AX_X, ALU.max).then_inc(*dve.tell())
                    v.wait_ge(*dve.own())
                    tt(z.lg[:, :, 0:n], lp, z.red[:].unsqueeze(2).broadcast_to([P, NT, n]), ALU.subtract).then_inc(*dve.tell("expin"))
                    v.wait_ge(sems["expd"], dve.next("expd"))
                    total(n, z.pr)
                    tt(z.pr[:, :, 0:n], z.pr[:, :, 0:n], z.rinv[:].unsqueeze(2).broadcast_to([P, NT, n]), ALU.mult).then_inc(*dve.tell())
                    v.wait_ge(*dve.own())

                def total(n, src):
                    v.tensor_reduce(z.red[:], src[:, :, 0:n], AX_X, ALU.add).then_inc(*dve.tell())
                    v.wait_ge(*dve.own())
                    v.reciprocal(z.rinv[:], z.red[:]).then_inc(*dve.tell())
                    v.wait_ge(*dve.own())

                def scale_weights(n):
                    total(n, z.wtm)
                    tt(z.wtm[:, :, 0:n], z.wtm[:, :, 0:n], z.rinv[:].unsqueeze(2).broadcast_to([P, NT, n]), ALU.mult).then_inc(*dve.tell("wtm"))

                def split_weights(n):
                    v.wait_ge(sems["wT"], dve.next("wT"))
                    src, wsp, wres, wmid = z.bank[0:n, 1, :], z.wsp, z.wres, z.wmid
                    v.tensor_copy(wsp[0:n, :], src).then_inc(*dve.tell())
                    v.wait_ge(*dve.own())
                    tt(wres[0:n, :], src, wsp[0:n, :], ALU.subtract).then_inc(*dve.tell())
                    v.wait_ge(*dve.own())
                    v.tensor_copy(wmid[0:n, :], wres[0:n, :]).then_inc(*dve.tell())
                    v.wait_ge(*dve.own())
                    v.tensor_copy(wsp[32:32 + n, :], wmid[0:n, :]).then_inc(*dve.tell())
                    tt(wsp[64:64 + n, :], wres[0:n, :], wmid[0:n, :], ALU.subtract).then_inc(*dve.tell("wsplit"))

                def ffn(kind):
                    used0, up0 = dve.seen.get("used", 0), dve.seen.get("up", 0)
                    blocks = ffn_blocks(kind)
                    for i, (_, _, sel, _) in enumerate(blocks):
                        s = z.tanh[:, i % 2, :]
                        if sel is not None and kind != "moe2":
                            v.wait_ge(sems["bcast"], dve.next("bcast"))
                            if i:
                                v.wait_ge(sems["up"], dve.at("up", up0 + i))
                            tt(z.hw[:], h[:], B[1], ALU.mult).then_inc(*dve.tell("weighted"))
                        yield
                        v.wait_ge(sems["tanh"], dve.next("tanh"))
                        stt(s, s, 1.0, B[0], ALU.add, ALU.mult).then_inc(*dve.tell("gate_used"))
                        v.wait_ge(*dve.own())
                        if sel is not None and kind == "moe2":
                            v.wait_ge(sems["bcast"], dve.next("bcast"))
                            tt(s, s, B[1], ALU.mult).then_inc(*dve.tell("weighted"))
                            v.wait_ge(*dve.own())
                        v.wait_ge(sems["up"], dve.at("up", up0 + i + 1))
                        if i >= 2:
                            v.wait_ge(sems["used"], dve.at("used", used0 + i - 1))
                        stt(z.gated[:, i % 2, :], s, 0.5, B[2], ALU.mult, ALU.mult).then_inc(*dve.tell("gated"))
                        yield
                    dve.seen["used"] = used0 + len(blocks) - 1
                    yield

                def attention(cfg):
                    chunk, causal = cfg["chunk"], cfg["causal"]
                    sides = 1 if chunk else 2
                    for side in range(sides):
                        bias = cfg["bq"] if side == 0 else cfg["bk"]
                        part, rest = z.parts[:, side], z.residue[:, side, :]
                        v.wait_ge(sems["part1"], dve.next("part1"))
                        if bias is None:
                            tt(rest, B[side], part[:, 0, :], ALU.subtract).then_inc(*dve.tell())
                        else:
                            stt(rest, B[side], bias, part[:, 0, :], ALU.add, ALU.subtract).then_inc(*dve.tell())
                        v.wait_ge(*dve.own())
                        v.tensor_copy(part[:, 1, :], rest).then_inc(*dve.tell())
                        v.wait_ge(*dve.own())
                        tt(part[:, 2, :], rest, part[:, 1, :], ALU.subtract).then_inc(*dve.tell())
                    yield
                    v.wait_ge(sems["vtm"], dve.next("vtm"))
                    if chunk:
                        vt = B[2].rearrange("p (i k j d) -> p i k j d", i=NT, k=NT, j=4)
                        vd = z.Vp[:, :, :, :].rearrange("p k (i c) w -> p k i c w", c=4)
                        for c in range(4):
                            for j in range(4):
                                v.tensor_copy(
                                    vd[32 * j:32 * j + 32, :, :, c, 0:HD].rearrange("p k i d -> p i k d"),
                                    vt[32 * c:32 * c + 32, :, :, j, :]).then_inc(*dve.tell("vready"))
                    else:
                        v.tensor_copy(z.Vp[:, :, :, 0:HD], B[2].rearrange("p (t h d) -> p t h d", t=NT, d=HD)).then_inc(*dve.tell("vready"))
                    yield from idle(SPLITTING - 1 + STACKING)
                    for n in range(UNITS * NT):
                        u, qt = divmod(n, NT)
                        if causal:
                            v.wait_ge(sems["sc1"], dve.next("sc1"))
                            v.tensor_reduce(z.mx[:, qt, u:u + 1], B[n % 4][:, 0:P * (qt + 1)], AX_X, ALU.max).then_inc(*dve.tell("bank_read"))
                        elif n % 2:
                            v.wait_ge(sems["sc1"], dve.next("sc1"))
                            v.tensor_reduce(z.mx[:, qt - 1:qt + 1, u], z.bank[:, n % 4 - 1:n % 4 + 1, :], AX_X, ALU.max).then_inc(*dve.tell("bank_read"))
                        if n % 4 == 3:
                            yield
                    v.wait_ge(sems["mT"], dve.next("mT"))
                    r = slice(0, 64) if chunk else slice(0, UNITS)
                    cols = slice(0, P) if chunk else slice(0, S)
                    ts(z.msp[r, 0, cols], B[0][r, cols], -1.0, None, ALU.mult, None).then_inc(*dve.tell())
                    v.wait_ge(*dve.own())
                    stt(z.msp[r, 1, cols], B[0][r, cols], -1.0, z.msp[r, 0, cols], ALU.mult, ALU.subtract).then_inc(*dve.tell("msplit"))
                    yield from idle(MAXIMA)
                    pv0 = dve.seen.get("pv", 0)
                    for g in range(GROUPS):
                        if g:
                            v.wait_ge(sems["pv"], dve.at("pv", pv0 + NT * g))
                            v.tensor_copy(z.osum[:, g - 1, :], B[3]).then_inc(*dve.tell("bank_read"))
                        yield from idle(NT)
                    v.wait_ge(sems["pv"], dve.at("pv", pv0 + NT * GROUPS))
                    v.tensor_copy(z.osum[:, GROUPS - 1, :], B[3]).then_inc(*dve.tell("bank_read"))
                    yield
                    v.wait_ge(sems["den"], dve.next("den"))
                    v.reciprocal(z.rinv16[:, :, :, :].rearrange("p g t c -> p (g t c)"), B[2][:, 0:UNITS * NT]).then_inc(*dve.tell("rden"))
                    yield
                    for g in range(GROUPS):
                        v.wait_ge(sems["dbroad"], dve.next("dbroad"))
                        tt(z.osum[:, g, :], z.osum[:, g, :], B[g], ALU.mult).then_inc(*dve.tell("onorm"))
                    yield

                def rms(gain, finish):
                    yield from idle(2)
                    v.wait_ge(sems["var"], dve.next("var"))
                    rsqrt(4, 1e-5)
                    yield
                    v.wait_ge(sems["rbroad"], dve.next("rbroad"))
                    v.wait_ge(sems["copied"], dve.next("copied"))
                    stt(ta[:], ta[:], gain, B[2], ALU.mult, ALU.mult).then_inc(*dve.tell())
                    v.wait_ge(*dve.own())
                    finish()
                    yield

                yield from layernorm(x[:], h[:], first=True)
                yield from layernorm(h[:], acc[:], gain=V["L0_attn_ln_g"], bias=V["L0_attn_ln_b"])
                yield
                turned = (B[3], B[0])
                for k, src in enumerate((ta, tb)):
                    v.wait_ge(sems["copied"], dve.next("copied"))
                    tt(z.gated[:, k, :], src[:], C["cos"], ALU.mult).then_inc(*dve.tell())
                    v.wait_ge(sems["turned"], dve.next("turned"))
                    tt(z.residue[:, k, :], turned[k], C["sin"], ALU.mult).then_inc(*dve.tell())
                    v.wait_ge(*dve.own())
                    tt(z.residue[:, k, :], z.residue[:, k, :], z.gated[:, k, :], ALU.add).then_inc(*dve.tell("rotated"))
                yield
                v.wait_ge(sems["var"], dve.next("var"))
                rsqrt(8, 1e-6)
                yield
                v.wait_ge(sems["rbroad"], dve.next("rbroad"))
                tt(tb[:], z.residue[:, 1, :], B[3], ALU.mult).then_inc(*dve.tell())
                v.wait_ge(sems["copied"], dve.next("copied"))
                v.wait_ge(*dve.own())
                v.tensor_tensor_reduce(tb[:], tb[:], z.vsb, 1.0, 0.0, ALU.mult, ALU.add, z.unit1[:]).then_inc(*dve.tell())
                v.wait_ge(*dve.own())
                stt(ta[:], z.residue[:, 0, :], z.unit1[:], B[2], ALU.mult, ALU.mult).then_inc(*dve.tell("y"))
                yield
                v.wait_ge(sems["yout"], dve.next("yout"))
                tt(ta[:], h[:], B[0], ALU.add).then_inc(*dve.tell())
                v.wait_ge(*dve.own())
                tt(x[:], x[:], ta[:], ALU.add).then_inc(*dve.tell("resid"))
                yield

                yield from layernorm(x[:], h[:])
                v.wait_ge(sems["logits"], dve.next("logits"))
                v.tensor_copy(z.lg[:, :, 0:8], z.bank[:, 0, 0:32].rearrange("p (t e) -> p t e", t=NT)).then_inc(*dve.tell())
                v.wait_ge(*dve.own())
                yield from top(8, 1, z.lg)
                ts(z.wtm[:, :, 0:8], z.rank[:, :, 0:8], 1.0, None, ALU.is_lt, None).then_inc(*dve.tell("wtm"))
                yield
                split_weights(8)
                v.wait_ge(*dve.own())
                v.tensor_copy(z.onehot[0:8, :], z.wsp[0:8, :]).then_inc(*dve.tell("y"))
                yield
                used0 = dve.seen.get("maskused", 0)
                for e in range(8):
                    v.wait_ge(sems["bcast"], dve.next("bcast"))
                    if e >= 2:
                        v.wait_ge(sems["maskused"], dve.at("maskused", used0 + e - 1))
                    tt(z.gated[:, e % 2, :], h[:], B[e % 2], ALU.mult).then_inc(*dve.tell("masked"))
                    yield
                dve.seen["maskused"] = used0 + 7
                v.wait_ge(sems["out0"], dve.next("out0"))
                tt(x[:], x[:], B[3], ALU.add).then_inc(*dve.tell("resid"))
                yield

                yield from layernorm(x[:], h[:])
                yield from attention(ATTN["chunk"])
                yield from idle(1 + OUTPUTS)
                v.wait_ge(sems["yout"], dve.next("yout"))
                stt(x[:], B[0], V["L1_attn_bu"], x[:], ALU.add, ALU.add).then_inc(*dve.tell("resid"))
                yield

                yield from layernorm(x[:], h[:])
                yield from attention(ATTN["causal"])
                yield from rms(V["L1_ffn_attn_norm_w"],
                               lambda: tt(acc[:], ta[:], h[:], ALU.add).then_inc(*dve.tell("y")))
                softmax(8)
                yield from top(8, 2, z.pr, "wtm")
                yield
                split_weights(8)
                yield
                yield from ffn("dense")
                yield from rms(V["L1_ffn_ff_norm_w"],
                               lambda: tt(tb[:], ta[:], acc[:], ALU.add).then_inc(*dve.tell("y")))
                yield from ffn("moe1")

                def finish():
                    tt(tb[:], tb[:], ta[:], ALU.add).then_inc(*dve.tell())
                    v.wait_ge(*dve.own())
                    tt(x[:], x[:], tb[:], ALU.add).then_inc(*dve.tell("resid"))

                yield from rms(V["L1_ffn_moe_norm_w"], finish)

                yield from layernorm(x[:], h[:])
                for src, e, bias in ((B[0], z.qe[:], V["L2_attn_bq"]), (B[1], z.ke[:], V["L2_attn_bk"]),
                                     (B[2], xc[:], None)):
                    v.wait_ge(sems["l2act"], dve.next("l2act"))
                    ts(e, e, 1.0, -1.0, ALU.min, ALU.add).then_inc(*dve.tell())
                    v.wait_ge(*dve.own())
                    if bias is None:
                        stt(e, src, 0.0, e, ALU.max, ALU.add).then_inc(*dve.tell("l2dve"))
                    else:
                        ts(tb[:], src, bias, 0.0, ALU.add, ALU.max).then_inc(*dve.tell())
                        v.wait_ge(*dve.own())
                        tt(e, tb[:], e, ALU.add).then_inc(*dve.tell("l2dve"))
                yield
                v.wait_ge(sems["l2act"], dve.next("l2act"))
                ts(z.vtanh[:], z.vtanh[:], 0.5, 0.5, ALU.mult, ALU.add).then_inc(*dve.tell())
                v.wait_ge(*dve.own())
                tt(z.vtm, z.vtanh[:], B[3], ALU.mult).then_inc(*dve.tell("l2dve"))
                yield
                v.wait_ge(*dve.own())
                v.wait_ge(sems["l2z"], dve.at("l2z", 1))
                flat = z.Vz.rearrange("p t h d -> p t (h d)")
                vh = z.vtm.rearrange("p (t h d) -> p t h d", t=NT, d=16)
                v.tensor_copy(flat[:, :, 0:7 * 144].rearrange("p t (h w) -> p t h w", w=144)[:, :, :, 0:16],
                              vh[:, :, 0:7, :]).then_inc(*dve.tell("l2dve"))
                v.tensor_copy(flat[:, :, 7 * 144:8 * P], vh[:, :, 7, :]).then_inc(*dve.tell("l2dve"))
                v.wait_ge(sems["l2act"], dve.next("l2act"))
                ts(z.utanh, z.utanh, 0.5, 0.5, ALU.mult, ALU.add).then_inc(*dve.tell())
                v.wait_ge(*dve.own())
                stt(z.uu[:], B[0], V["L2_attn_bu"], z.utanh, ALU.add, ALU.mult).then_inc(*dve.tell("l2dve"))
                yield
                for j in range(NT - 1):
                    for hh in range(3 * j, min(3 * j + 3, 8)):
                        ts(z.Kh[:, hh, :], z.ke[:], C["head"][:, hh:hh + 1], None, ALU.mult, None).then_inc(*dve.tell("l2dve"))
                    v.wait_ge(sems["state"], dve.next("state"))
                    tt(z.state[:, j, :], B[1][:, 0:P], C["block"], ALU.mult).then_inc(*dve.tell("statesb"))
                    yield from idle(SPREAD)
                em0 = dve.seen.get("maskused", 0)
                tril = C["tril"].unsqueeze(1).broadcast_to([P, 4, P])
                for n in range(2 * NT):
                    v.wait_ge(sems["energy"], dve.next("energy"))
                    if n >= 2:
                        v.wait_ge(sems["maskused"], dve.at("maskused", em0 + n - 1))
                    tt(z.energy[:, n % 2, :].rearrange("p (a b) -> p a b", a=4), tril,
                       (B[0] if n % 2 else B[2]).rearrange("p (a b) -> p a b", a=4), ALU.mult).then_inc(*dve.tell("masked"))
                    yield from idle(SPREAD)
                yield from idle(3)
                v.wait_ge(sems["var"], dve.next("var"))
                rsqrt(4, 0.0, None)
                v.wait_ge(*dve.own())
                tt(stat[:, 16:20], stat[:, 0:4], stat[:, 8:12], ALU.mult).then_inc(*dve.tell())
                v.wait_ge(*dve.own())
                ts(stat[:, 16:20], stat[:, 16:20], 1e-8, None, ALU.add, None).then_inc(*dve.tell())
                v.wait_ge(*dve.own())
                v.reciprocal(stat[:, 8:12], stat[:, 16:20]).then_inc(*dve.tell("rstd"))
                yield
                v.wait_ge(sems["rbroad"], dve.next("rbroad"))
                v.wait_ge(sems["copied"], dve.next("copied"))
                stt(ta[:], ta[:], V["L2_attn_scale"], B[2], ALU.mult, ALU.mult).then_inc(*dve.tell())
                v.wait_ge(*dve.own())
                tt(ta[:], ta[:], z.uu[:], ALU.mult).then_inc(*dve.tell("y"))
                yield
                v.wait_ge(sems["yout"], dve.next("yout"))
                stt(x[:], B[0], V["L2_attn_bo"], x[:], ALU.add, ALU.add).then_inc(*dve.tell("resid"))
                yield

                yield from layernorm(x[:], h[:])
                v.wait_ge(sems["logits"], dve.next("logits"))
                v.wait_ge(sems["expd"], dve.next("expd"))
                ts(z.pr[:, :, 0:16], z.pr[:, :, 0:16], 0.5, 0.5, ALU.mult, ALU.add).then_inc(*dve.tell())
                v.wait_ge(*dve.own())
                yield from top(16, 4, z.pr)
                scale_weights(16)
                yield
                split_weights(16)
                yield
                yield from ffn("moe2")
                v.wait_ge(sems["moe2_out"], dve.next("moe2_out"))
                tt(x[:], x[:], B[3], ALU.add).then_inc(*dve.tell("resid"))

                yield from layernorm(x[:], h[:])
                yield from attention(ATTN["full"])
                v.wait_ge(sems["yout"], dve.next("yout"))
                stt(x[:], B[0], V["L3_attn_bo"], x[:], ALU.add, ALU.add).then_inc(*dve.tell("resid"))
                yield
                yield from layernorm(x[:], h[:])
                softmax(8)
                yield from top(8, 2, z.pr)
                scale_weights(8)
                yield
                split_weights(8)
                yield
                yield from ffn("moe3")
                v.wait_ge(sems["moe3_out"], dve.next("moe3_out"))
                tt(x[:], x[:], B[3], ALU.add).then_inc(*dve.tell("resid"))
                yield

            ahead, when = begin_turns(stream)
            v.wait_ge(shared["w_loaded"], 16 * n_loads)
            v.wait_ge(shared["zeroed"], ZEROED)
            v.wait_ge(shared["consts"], FILLS)
            for dst, n in ((identb, "ident"), (upperb, "upper"), (lowerb, "lower"),
                           (selb[:, :, :].rearrange("p a b -> p (a b)"), "sel"),
                           (stackb[:, :, :, :, :].rearrange("p g s a m -> p (g s a m)"), "stack"),
                           (pairb[:, :, :].rearrange("p a b -> p (a b)"), "pair")):
                v.tensor_copy(dst[:] if n in ("ident", "upper", "lower") else dst, C[n]).then_inc(shared["consts"], 1)
            v.tensor_scalar(half_bu, V["L2_attn_bu"], 0.5, None, ALU.mult).then_inc(shared["consts"], 1)
            with v.Fori(0, TURNS) as turn:
                ahead, when = run_turn(stream, ahead, when, turn)

        @block.tensor
        def _(t_eng):
            t_eng.wait_ge(shared["first_loaded"], 16 * len(first_loads))

            def mm(out, lhsT, rhs, start=True, stop=True, **kw):
                return t_eng.matmul(out, lhsT, rhs, start=start, stop=stop, **kw)

            def stream(i, when):
                z = Z[i]
                sems = z.sems
                pe = Count(sems, None, when, i)
                counts.setdefault(("pe", i), pe)
                B = [z.bank[:, k, :] for k in range(4)]
                h, wsp = z.h, z.wsp
                stat = z.stat[:, :, :].rearrange("p a b -> p (a b)")

                def squares(tiles):
                    for k, (src, column) in enumerate(tiles):
                        for t in range(NT):
                            ins = mm(B[1][:, NT * k + t:NT * k + t + 1], src[:, P * t:P * t + P], column)
                    ins.then_inc(*pe.tell("var"))

                def spread_rstd(bank, k=0, name="rbroad"):
                    for t in range(NT):
                        c = 8 + NT * k + t
                        ins = mm(bank[:, P * t:P * t + P], stat[:, c:c + 1].broadcast_to([P, P]), C["ident"])
                    if name:
                        ins.then_inc(*pe.tell(name))

                def layernorm(src, ready, n=1):
                    if ready:
                        t_eng.wait_ge(sems[ready], pe.next(ready, n))
                    mm(B[0], C["mean"], src).then_inc(*pe.tell("mean"))
                    yield
                    t_eng.wait_ge(sems["squared"], pe.next("squared"))
                    squares([(z.sq, C["mean"][:, 0:1])])
                    yield from idle(2)
                    t_eng.wait_ge(sems["rstd"], pe.next("rstd"))
                    spread_rstd(B[0])
                    yield
                    t_eng.wait_ge(sems["normed"], pe.next("normed"))

                def rms():
                    yield
                    t_eng.wait_ge(sems["squared"], pe.next("squared"))
                    squares([(z.sq, C["mean"][:, 0:1])])
                    yield from idle(2)
                    t_eng.wait_ge(sems["rstd"], pe.next("rstd"))
                    spread_rstd(B[2])
                    yield
                    t_eng.wait_ge(sems["y"], pe.next("y"))

                def route(n, weights, bias=None):
                    for t in range(NT):
                        out = z.bank[:, 0, n * t:n * t + n]
                        ins = mm(out, h[:, P * t:P * t + P], weights, stop=bias is None)
                        if bias is not None:
                            ins = mm(out, C["ones"][0:1, :], bias, start=False)
                    ins.then_inc(*pe.tell("logits"))
                    yield from idle(ROUTE - 1)
                    t_eng.wait_ge(sems["wtm"], pe.next("wtm"))
                    for t in range(NT):
                        ins = t_eng.transpose(z.bank[0:n, 1, P * t:P * t + P], z.wtm[:, t, 0:n], C["ident"])
                    ins.then_inc(*pe.tell("wT"))
                    yield
                    t_eng.wait_ge(sems["wsplit"], pe.next("wsplit"))

                def ffn(kind, rhs):
                    blocks = ffn_blocks(kind)
                    weighted0, used0, gated0 = pe.seen.get("weighted", 0), pe.seen.get("gate_used", 0), pe.seen.get("gated", 0)
                    experts = 0
                    for i, (w1, w3, sel, _) in enumerate(blocks):
                        if sel is not None:
                            if experts:
                                t_eng.wait_ge(sems["weighted"], pe.at("weighted", weighted0 + experts))
                            mm(B[1], sel, wsp[:, :]).then_inc(*pe.tell("bcast"))
                            experts += 1
                        if i:
                            t_eng.wait_ge(sems["gate_used"], pe.at("gate_used", used0 + i))
                        mm(B[0], w1, rhs).then_inc(*pe.tell("gate"))
                        yield
                        if i:
                            t_eng.wait_ge(sems["gated"], pe.at("gated", gated0 + i))
                        if experts and kind != "moe2":
                            t_eng.wait_ge(sems["weighted"], pe.at("weighted", weighted0 + experts))
                            mm(B[2], w3, z.hw[:]).then_inc(*pe.tell("up"))
                        else:
                            mm(B[2], w3, rhs).then_inc(*pe.tell("up"))
                        if i:
                            mm(B[3], blocks[i - 1][3], z.gated[:, (i - 1) % 2, :], start=i == 1, stop=False).then_inc(*pe.tell("used"))
                        yield
                    n = len(blocks)
                    t_eng.wait_ge(sems["gated"], pe.at("gated", gated0 + n))
                    mm(B[3], blocks[-1][3], z.gated[:, (n - 1) % 2, :], start=False).then_inc(*pe.tell(kind + "_out"))
                    pe.seen["gate_used"] = used0 + n
                    pe.seen["weighted"] = weighted0 + experts
                    yield

                def attention(cfg):
                    chunk, causal = cfg["chunk"], cfg["causal"]
                    mm(B[0], W[cfg["q"]][:], h[:]).then_inc(*pe.tell("proj"))
                    if not chunk:
                        mm(B[1], W[cfg["k"]][:], h[:]).then_inc(*pe.tell("proj"))
                    for t in range(NT):
                        out = B[2][:, P * t:P * t + P]
                        ins = mm(out, h[:, P * t:P * t + P], W[cfg["v"]][:], stop=cfg["bv"] is None)
                        if cfg["bv"] is not None:
                            ins = mm(out, C["ones"][0:1, :], cfg["bv"], start=False)
                    ins.then_inc(*pe.tell("vtm"))
                    yield from idle(SPLITTING)
                    t_eng.wait_ge(sems["vready"], pe.next("vready", 16 if chunk else 1))
                    stacked0 = pe.seen.get("stacked", 0)
                    for n in range(UNITS):
                        pair, side = divmod(n, 2)
                        if n >= 4:
                            t_eng.wait_ge(sems["stacked"], pe.at("stacked", stacked0 + 3 * (pair - 2) + 1 + 2 * side))
                        picks = stackb[:, pair, side]
                        parts = z.parts[:, 0 if chunk else side]
                        if chunk:
                            for half in range(2):
                                for odd in range(2):
                                    for a in range(3):
                                        ins = mm(B[n % 4][64 * odd:64 * odd + 64, 256 * half:256 * half + 256],
                                                 picks[:, a, 64 * half:64 * half + 64],
                                                 parts[:, a, :].rearrange("p (c two t) -> p two c t", two=2, t=32)[:, odd],
                                                 start=a == 0, stop=a == 2)
                        else:
                            for a in range(3):
                                ins = mm(B[n % 4], picks[:, a, :], parts[:, a, :], start=a == 0, stop=a == 2)
                        ins.then_inc(*pe.tell("raised"))
                        if side:
                            yield
                    t_eng.wait_ge(sems["stacked"], pe.at("stacked", stacked0 + 3 * UNITS // 2))
                    read0 = pe.seen.get("bank_read", 0)
                    shared_by = 1 if causal else 2
                    maxima = UNITS * NT // shared_by
                    for n in range(UNITS * NT):
                        u, qt = divmod(n, NT)
                        keys = P * (qt + 1) if causal else S
                        if n >= 4 and n % shared_by == 0:
                            t_eng.wait_ge(sems["bank_read"], pe.at("bank_read", read0 + (n - 4) // shared_by + 1))
                        ins = mm(B[n % 4][:, 0:keys], q_stack(z, u)[:, P * qt:P * qt + P], k_stack(z, u)[:, 0:keys], stop=not causal)
                        if causal:
                            ins = mm(B[n % 4][:, keys - P:keys], identb[:], upperb[:], start=False)
                        if n % shared_by == shared_by - 1:
                            ins.then_inc(*pe.tell("sc1"))
                        if n % 4 == 3:
                            yield
                    t_eng.wait_ge(sems["bank_read"], pe.at("bank_read", read0 + maxima))
                    t_eng.sem_inc(shared["paced"], 1)
                    if chunk:
                        ins = t_eng.transpose(z.bank[0:64, 0, 0:P], z.mx[:, :, :].rearrange("p a b -> p (a b)"), C["ident"])
                    else:
                        for t in range(NT):
                            ins = t_eng.transpose(z.bank[0:UNITS, 0, P * t:P * t + P], z.mx[:, t, :], C["ident"])
                    ins.then_inc(*pe.tell("mT"))
                    yield from idle(MAXIMA)
                    t_eng.wait_ge(sems["mstacked"], pe.next("mstacked", 32))
                    prob0 = pe.seen.get("prob", 0)
                    slots = 0

                    def sums(n):
                        g, kt = divmod(n, NT)
                        q = qcols(kt, causal)
                        t_eng.wait_ge(sems["prob"], pe.at("prob", prob0 + 4 * n + 4))
                        if kt == 0 and g:
                            t_eng.wait_ge(sems["bank_read"], pe.at("bank_read", read0 + maxima + g))
                        for c in range(4):
                            ins = mm(B[3][32 * c:32 * c + 32, q], z.Vp[:, kt, 4 * g + c, :],
                                     z.probs[:, 4 * (n % 2) + c, q], start=kt == 0, stop=kt == NT - 1)
                        ins.then_inc(*pe.tell("pv"))

                    for n in range(GROUPS * NT):
                        g, kt = divmod(n, NT)
                        q = qcols(kt, causal)
                        for c in range(4):
                            if slots >= 3:
                                t_eng.wait_ge(sems["prob"], pe.at("prob", prob0 + slots - 2))
                            bank = B[slots % 3]
                            slots += 1
                            u = 4 * g + c
                            ins = mm(bank[:, q], k_stack(z, u)[:, P * kt:P * kt + P], q_stack(z, u)[:, q], stop=not causal)
                            if causal:
                                ins = mm(bank[:, P * kt:P * kt + P], identb[:], lowerb[:], start=False)
                            ins.then_inc(*pe.tell("sc2"))
                            if c == 2 and n:
                                sums(n - 1)
                        yield
                    sums(GROUPS * NT - 1)
                    yield
                    t_eng.wait_ge(sems["bank_read"], pe.at("bank_read", read0 + maxima + GROUPS))
                    for g in range(GROUPS):
                        for t in range(NT):
                            c0 = UNITS * g + 4 * t
                            ins = mm(B[2][:, c0:c0 + 4], z.osum[:, g, P * t:P * t + P], C["den"])
                    ins.then_inc(*pe.tell("den"))
                    yield
                    for g in range(GROUPS):
                        t_eng.wait_ge(sems["widened"], pe.next("widened"))
                        for t in range(NT):
                            ins = mm(B[g][:, P * t:P * t + P], z.probs[:, g, P * t:P * t + P], C["ident"])
                        ins.then_inc(*pe.tell("dbroad"))
                    yield
                    t_eng.wait_ge(sems["onorm"], pe.next("onorm", GROUPS))

                def project(weights, name):
                    for g in range(GROUPS):
                        ins = mm(B[0], weights[:, g, :], z.osum[:, g, :], start=g == 0, stop=g == GROUPS - 1)
                    ins.then_inc(*pe.tell(name))

                yield from layernorm(z.x[:], "x_loaded", 16)
                yield from layernorm(h[:], None)
                for k in range(3):
                    mm(B[k], W["in0"][:, P * k:P * k + P], z.acc[:]).then_inc(*pe.tell("qkv"))
                yield
                t_eng.wait_ge(sems["copied"], pe.next("copied"))
                mm(B[3], C["rot"], z.ta[:]).then_inc(*pe.tell("turned"))
                t_eng.wait_ge(sems["copied"], pe.next("copied", 2))
                mm(B[0], C["rot"], z.tb[:]).then_inc(*pe.tell("turned"))
                yield
                t_eng.wait_ge(sems["squared"], pe.next("squared", 2))
                squares([(z.sq, C["ones"][:, 0:1]), (z.xc, C["ones"][:, 0:1])])
                yield
                t_eng.wait_ge(sems["rstd"], pe.next("rstd"))
                spread_rstd(B[2], 0, None)
                spread_rstd(B[3], 1)
                yield
                t_eng.wait_ge(sems["y"], pe.next("y"))
                mm(B[0], W["out0"][:], z.ta[:]).then_inc(*pe.tell("yout"))
                yield
                yield from layernorm(z.x[:], "resid")
                yield from route(8, W["gate0"][:], RB["L0_ffn_gate_b"])
                t_eng.wait_ge(sems["y"], pe.next("y"))
                mm(B[3], W["expb0"][:], z.onehot[0:8, :], stop=False)
                m0 = pe.seen.get("masked", 0)
                for e in range(9):
                    if e < 8:
                        if e >= 2:
                            t_eng.wait_ge(sems["masked"], pe.at("masked", m0 + e - 1))
                        mm(B[e % 2], selb[0:96, e, :], wsp[:, :]).then_inc(*pe.tell("bcast"))
                    if e >= 1:
                        t_eng.wait_ge(sems["masked"], pe.at("masked", m0 + e))
                        mm(B[3], W["exp0"][:, e - 1, :], z.gated[:, (e - 1) % 2, :], start=False, stop=e == 8).then_inc(*pe.tell("out0" if e == 8 else "maskused"))
                    yield
                yield from layernorm(z.x[:], "resid")
                yield from attention(ATTN["chunk"])
                yield from idle(1 + OUTPUTS)
                t_eng.wait_ge(sems["oback"], pe.next("oback", 16))
                mm(B[0], W["u1"][:], z.outT[:]).then_inc(*pe.tell("yout"))
                yield
                yield from layernorm(z.x[:], "resid")
                yield from attention(ATTN["causal"])
                project(padded["of"], "attn_out")
                yield from rms()
                yield from route(8, W["routef"][:])
                t_eng.wait_ge(sems["window"], pe.at("window", IN_WINDOW[0]))
                yield from ffn("dense", z.acc[:])
                yield from rms()
                yield from ffn("moe1", h[:])
                yield
                t_eng.wait_ge(sems["squared"], pe.next("squared"))
                squares([(z.sq, C["mean"][:, 0:1])])
                yield from idle(2)
                t_eng.wait_ge(sems["rstd"], pe.next("rstd"))
                spread_rstd(B[2])
                yield
                yield from layernorm(z.x[:], "resid")
                mm(B[0], W["q2"][:], h[:]).then_inc(*pe.tell("l2a"))
                mm(B[1], W["k2"][:], h[:]).then_inc(*pe.tell("l2a"))
                for bank, n, bias in ((B[2], "k2", RB["L2_attn_bk"]), (B[3], "v2", RB["L2_attn_bv"])):
                    for t in range(NT):
                        out = bank[:, P * t:P * t + P]
                        mm(out, h[:, P * t:P * t + P], W[n][:], stop=False)
                        ins = mm(out, C["ones"][0:1, :], bias, start=False)
                    ins.then_inc(*pe.tell("l2a"))
                yield from idle(2)
                t_eng.wait_ge(sems["l2dve"], pe.next("l2dve"))
                mm(B[0], W["u2"][:], h[:]).then_inc(*pe.tell("l2a"))
                yield
                t_eng.wait_ge(sems["l2dve"], pe.next("l2dve", 3))
                for j in range(NT - 1):
                    if j:
                        t_eng.wait_ge(sems["statesb"], pe.next("statesb"))
                    mm(B[1][:, 0:P], z.ktm[:, j, :], z.vtm[:, P * j:P * j + P], start=j == 0, stop=True,
                       skip_group_check=True).then_inc(*pe.tell("state"))
                    yield from idle(SPREAD)
                t_eng.wait_ge(sems["statesb"], pe.next("statesb"))
                t_eng.wait_ge(sems["l2dve"], pe.next("l2dve", 11))

                def energies(n):
                    i, half = divmod(n, 2)
                    bank = B[0] if n % 2 else B[2]
                    for q in range(4):
                        ins = mm(bank[:, P * q:P * q + P], z.Kh[:, 4 * half + q, P * i:P * i + P], z.qe[:, P * i:P * i + P])
                    ins.then_inc(*pe.tell("energy"))

                em0 = pe.seen.get("masked", 0)
                for n in range(2 * NT + 1):
                    if n < 2 * NT:
                        if n >= 2:
                            t_eng.wait_ge(sems["masked"], pe.at("masked", em0 + n - 1))
                        energies(n)
                    if n:
                        m = n - 1
                        i, half = divmod(m, 2)
                        out = B[3][:, P * i:P * i + P]
                        if half == 0 and i > 0:
                            mm(out, z.state[:, i - 1, :], z.qe[:, P * i:P * i + P], stop=False)
                        t_eng.wait_ge(sems["masked"], pe.at("masked", em0 + m + 1))
                        for q in range(4):
                            ins = mm(out, z.Vz[:, i, 4 * half + q, :], z.energy[:, m % 2, P * q:P * q + P],
                                     start=half == 0 and q == 0 and i == 0, stop=half == 1 and q == 3)
                        ins.then_inc(*pe.tell("l2out" if m == 2 * NT - 1 else "maskused"))
                    yield from idle(SPREAD if n < 2 * NT else 1)
                yield from rms()
                mm(B[0], W["o2"][:], z.ta[:]).then_inc(*pe.tell("yout"))
                yield
                yield from layernorm(z.x[:], "resid")
                yield from route(16, W["gate2"][:])
                t_eng.wait_ge(sems["window"], pe.at("window", IN_WINDOW[1]))
                yield from ffn("moe2", h[:])
                yield from layernorm(z.x[:], "resid")
                yield from attention(ATTN["full"])
                project(padded["o3"], "yout")
                yield
                yield from layernorm(z.x[:], "resid")
                yield from route(8, W["gate3"][:])
                t_eng.wait_ge(sems["window"], pe.at("window", IN_WINDOW[2]))
                yield from ffn("moe3", h[:])
                yield

            ahead, when = begin_turns(stream)
            t_eng.wait_ge(shared["w_loaded"], 16 * n_loads)
            t_eng.wait_ge(shared["consts"], CONSTS_READY)
            with t_eng.Fori(0, TURNS) as turn:
                ahead, when = run_turn(stream, ahead, when, turn)

        made = {}
        for (engine, i), count in counts.items():
            if i != 1:
                for n, k in count.made.items():
                    made[n] = made.get(n, 0) + k
        return made


_TURNED = ["L0_attn_W_in", "L0_attn_W_out", "L1_attn_wq", "L1_attn_wu", "L2_attn_Wq", "L2_attn_Wk", "L2_attn_Wv",
           "L2_attn_Wu", "L2_attn_Wo", "L2_ffn_gate_w", "L3_attn_Wo", "L3_ffn_gate_w"]
_HEADS = ["L3_attn_Wq", "L3_attn_Wk", "L3_attn_Wv"]
_EXPERTS = ["L3_ffn_w1", "L3_ffn_w2", "L3_ffn_w3"]
_FLAT = ["L3_attn_bq", "L3_attn_bk", "L3_attn_bv"]


def kernel(**inputs):
    import numpy as _np
    import concourse.bacc as _bacc
    from concourse import mybir as _mybir
    from concourse.bass_utils import run_bass_kernel_spmd as _run

    nc = _bacc.Bacc("TRN2", target_bir_lowering=False, num_devices=1)
    arrays, args = {}, {}

    def declare(name, a):
        a = _np.ascontiguousarray(a)
        arrays["in_" + name] = a
        return nc.dram_tensor("in_" + name, a.shape, _mybir.dt.from_np(a.dtype), kind="ExternalInput").ap()

    for name, a in inputs.items():
        a = _np.asarray(a)
        if name == "L0_attn_X":
            x_in = declare(name, a.transpose(0, 2, 1))
            continue
        if name in _TURNED:
            a = a.T
        elif name in _HEADS:
            a = a.reshape(P, P).T
        elif name in _EXPERTS:
            a = a.transpose(2, 0, 1)
        elif name in _FLAT:
            a = a.reshape(P)
        args[name] = declare(name, a)
    const = declare("constants", constant_table())
    x_out = nc.dram_tensor("out_0", (NB, P, S), _mybir.dt.float32, kind="ExternalOutput").ap()
    made = network(nc, args, const, x_in, x_out)
    assert made == EVENTS, made
    r = _run(nc, [arrays], core_ids=[0])
    return _np.ascontiguousarray(r.results[0]["out_0"].transpose(0, 2, 1))
```
